# Optimizing a Trainium2 kernel written in Bass

```python
import numpy as np
import jax
import jax.numpy as jnp

def _softmax(x, axis=-1):
    return jax.nn.softmax(x, axis=axis)

def _gelu(x):
    return jax.nn.gelu(x, approximate=True)

def _silu(x):
    return jax.nn.silu(x)

def _sigmoid(x):
    return jax.nn.sigmoid(x)

def _layernorm(x, axis=-1, eps=1e-05):
    m = jnp.mean(x, axis=axis, keepdims=True)
    v = jnp.var(x, axis=axis, keepdims=True)
    return (x - m) / jnp.sqrt(v + eps)

def _scatter_add(tgt, idx, src, axis=0):
    return tgt.at[idx].add(src)

def _segment_sum(src, seg, n):
    return jax.ops.segment_sum(src, seg, n)
kernel_name = 'mk_adj_preln_d2_adj_r2_9e13d1'

def setup_inputs(seed: int=0):
    np.random.seed(seed)
    _w = jnp.asarray

    def _rec_inputs():
        import jax
        import jax.numpy as jnp
        _gk = jax.random.key(seed)
        x = -0.000125 + 0.9999 * jax.random.normal(jax.random.fold_in(_gk, 1), (64, 128, 256), jnp.float32)
        _a = jax.random.bernoulli(jax.random.fold_in(_gk, 2), 0.0625, (128, 128))
        _a = jnp.logical_or(_a, jnp.swapaxes(_a, -1, -2))
        _a = jnp.logical_or(_a, jnp.eye(128, dtype=bool))
        _af = _a.astype(jnp.float32)
        adj = _af
        return (x, adj)
    x, adj = _rec_inputs()

    def _L0_gnn_setup():
        import jax, jax.numpy as jnp
        import numpy as np
        ALPHA = 0.2
        key = jax.random.key(seed)
        k0, k1, k2, k3 = jax.random.split(key, 4)
        B, N, C, F = (64, 512, 256, 256)
        x = jax.random.normal(k0, (B, N, C), dtype=jnp.float32)
        W = jax.random.normal(k1, (C, F), dtype=jnp.float32) * (1.414 / np.sqrt(C + F))
        a = jax.random.normal(k2, (2 * F, 1), dtype=jnp.float32) * (1.414 / np.sqrt(2 * F + 1))
        beta = jnp.ones((1,), dtype=jnp.float32)
        mask = (jax.random.uniform(k3, (N, N)) < 0.3).astype(jnp.float32)
        return {'x': x, 'W': W, 'a': a, 'beta': beta, 'mask': mask}
    _L0_gnn_all = _L0_gnn_setup()
    _L0_gnn_in = {k: v for k, v in _L0_gnn_all.items() if k in ('W', 'a', 'beta')}
    del _L0_gnn_all

    def _L1_gnn_setup():
        import jax, jax.numpy as jnp
        import numpy as np
        B, N, D, H = (16, 1025, 256, 8)
        LN_EPS = 1e-05

        def _make_mask(key, n):
            n_proto = n - 1
            adj = jax.random.bernoulli(key, 0.03, (n_proto, n_proto)).astype(jnp.float32)
            adj = jnp.clip(adj + adj.T + jnp.eye(n_proto, dtype=jnp.float32), 0.0, 1.0)
            mask = jnp.zeros((n, n), dtype=jnp.float32)
            mask = mask.at[0, :].set(1.0).at[:, 0].set(1.0)
            mask = mask.at[1:, 1:].set(adj)
            return mask
        key = jax.random.key(seed)
        ks = jax.random.split(key, 7)
        s = 1.0 / np.sqrt(D)
        return {'x': jax.random.normal(ks[0], (B, N, D), dtype=jnp.float32), 'w_qkv': jax.random.uniform(ks[1], (D, 3 * D), dtype=jnp.float32, minval=-s, maxval=s), 'w_proj': jax.random.uniform(ks[2], (D, D), dtype=jnp.float32, minval=-s, maxval=s), 'b_proj': jnp.zeros((D,), dtype=jnp.float32), 'ln_gamma': jnp.ones((D,), dtype=jnp.float32), 'ln_beta': jnp.zeros((D,), dtype=jnp.float32), 'attn_mask': _make_mask(ks[3], N)}
    _L1_gnn_all = _L1_gnn_setup()
    _L1_gnn_in = {k: v for k, v in _L1_gnn_all.items() if k in ('w_qkv', 'w_proj', 'b_proj', 'ln_gamma', 'ln_beta')}
    del _L1_gnn_all
    return {'x': x, 'adj': adj, 'L0_gnn_W': _L0_gnn_in['W'], 'L0_gnn_a': _L0_gnn_in['a'], 'L0_gnn_beta': _L0_gnn_in['beta'], 'L1_gnn_w_qkv': _L1_gnn_in['w_qkv'], 'L1_gnn_w_proj': _L1_gnn_in['w_proj'], 'L1_gnn_b_proj': _L1_gnn_in['b_proj'], 'L1_gnn_ln_gamma': _L1_gnn_in['ln_gamma'], 'L1_gnn_ln_beta': _L1_gnn_in['ln_beta']}

def reference(x, adj, L0_gnn_W, L0_gnn_a, L0_gnn_beta, L1_gnn_w_qkv, L1_gnn_w_proj, L1_gnn_b_proj, L1_gnn_ln_gamma, L1_gnn_ln_beta):
    import jax
    import jax.numpy as jnp

    def _L0_gnn_ref(x, W, a, beta, mask):
        import jax, jax.numpy as jnp
        import numpy as np
        ALPHA = 0.2
        F_ = W.shape[1]
        h = jnp.einsum('bnc,cf->bnf', x, W)
        a1, a2 = (a[:F_, 0], a[F_:, 0])
        s1 = jnp.einsum('bnf,f->bn', h, a1)
        s2 = jnp.einsum('bnf,f->bn', h, a2)
        e = jax.nn.leaky_relu(s1[:, :, None] + s2[:, None, :], negative_slope=ALPHA)
        e = e * mask[None, :, :]
        att = jax.nn.softmax(e, axis=2)
        h_prime = jnp.einsum('bij,bjf->bif', att, h)
        return jax.nn.elu(h_prime + beta * h)

    def _L1_gnn_ref(x, w_qkv, w_proj, b_proj, ln_gamma, ln_beta, attn_mask):
        import jax, jax.numpy as jnp
        import numpy as np
        B, N, D, H = (16, 1025, 256, 8)
        LN_EPS = 1e-05

        def _make_mask(key, n):
            n_proto = n - 1
            adj = jax.random.bernoulli(key, 0.03, (n_proto, n_proto)).astype(jnp.float32)
            adj = jnp.clip(adj + adj.T + jnp.eye(n_proto, dtype=jnp.float32), 0.0, 1.0)
            mask = jnp.zeros((n, n), dtype=jnp.float32)
            mask = mask.at[0, :].set(1.0).at[:, 0].set(1.0)
            mask = mask.at[1:, 1:].set(adj)
            return mask
        b, n, d = x.shape
        hd = d // H
        scale = hd ** (-0.5)
        qkv = (x @ w_qkv).reshape(b, n, 3, H, hd).transpose(2, 0, 3, 1, 4)
        q, k, v = (qkv[0], qkv[1], qkv[2])
        attn = jnp.einsum('bhnd,bhmd->bhnm', q, k) * scale
        attn = jnp.where(attn_mask[None, None] == 0, -jnp.inf, attn)
        attn = jax.nn.softmax(attn, axis=-1)
        o = jnp.einsum('bhnm,bhmd->bhnd', attn, v).transpose(0, 2, 1, 3).reshape(b, n, d)
        o = o @ w_proj + b_proj
        mu = jnp.mean(o, axis=-1, keepdims=True)
        var = jnp.mean(jnp.square(o - mu), axis=-1, keepdims=True)
        ln = (o - mu) * jax.lax.rsqrt(var + LN_EPS) * ln_gamma + ln_beta
        return o + ln
    h = jnp.maximum(_layernorm(x, axis=-1), 0.0)
    x = x + _L0_gnn_ref(h, L0_gnn_W, L0_gnn_a, L0_gnn_beta, adj)
    h = jnp.maximum(_layernorm(x, axis=-1), 0.0)
    x = x + _L1_gnn_ref(h, L1_gnn_w_qkv, L1_gnn_w_proj, L1_gnn_b_proj, L1_gnn_ln_gamma, L1_gnn_ln_beta, adj)
    return x

_drawn_inputs = setup_inputs


def setup_inputs(seed=0):
    import zlib

    import numpy as np

    out = dict(_drawn_inputs(seed))
    spreads = {'L1_gnn_b_proj': (0.0, 0.1), 'L1_gnn_ln_gamma': (1.0, 0.2), 'L1_gnn_ln_beta': (0.0, 0.1)}
    factors = {'L0_gnn_a': 4.057}
    for name, (base, spread) in spreads.items():
        noise = np.random.default_rng([zlib.crc32(name.encode()), seed]).standard_normal(out[name].shape)
        drawn = base * np.exp(spread * noise) if base else spread * noise
        out[name] = jnp.asarray(drawn.astype(out[name].dtype))
    for name, factor in factors.items():
        out[name] = (out[name] * factor).astype(out[name].dtype)
    return out
```

```python
from contextlib import ExitStack

import concourse.bass as bass
from concourse import mybir

ALU = mybir.AluOpType
ACT = mybir.ActivationFunctionType
AX_X = mybir.AxisListType.X
F32 = mybir.dt.float32
F32R = mybir.dt.float32r
F16 = mybir.dt.float16
BF16 = mybir.dt.bfloat16

P = 128
LN_EPS = 1e-5
LEAKY_SLOPE = 0.2
MASKED = -1e30

LOAD = 0
NORM0 = 1
GAT_IN = 2
GAT_OUT = 3
QK = 4
VALUES = 5
ATTEND = 6
FINISH = 7
LAST_LAG = FINISH


def gat_transformer(nc, x, adj, gat_w, gat_a, gat_beta, w_qkv, w_proj, b_proj, ln_gamma, ln_beta, out):
    B, N, D = x.shape
    C = D // P
    H = 8
    HD = D // H
    HC = P // HD
    SCALE = float(HD) ** -0.5
    PAIR = 2
    NG = B // PAIR
    TOK = PAIR * N
    GW = PAIR * D
    DS = D + 2
    STACK = 3 * HD
    assert N == P and C == 2 and NG > LAST_LAG

    with ExitStack() as ctx:
        def sb(name, shape, dt=F32):
            return ctx.enter_context(nc.sbuf_tensor(name, shape, dt))

        def bank(name):
            return ctx.enter_context(nc.psum_tensor(name, [P, 512], F32))

        def sem(name):
            return ctx.enter_context(nc.semaphore(name))

        def two(make, name, *args):
            return [make(f"{name}{i}", *args) for i in range(2)]

        ident = sb("ident", [P, P])
        ident_bf = sb("ident_bf", [P, P], BF16)
        adj_sb = sb("adj_sb", [P, N])
        mask_add = sb("mask_add", [P, N], BF16)
        mask_add_t = sb("mask_add_t", [P, N], BF16)
        wx = sb("wx", [P, C, DS])
        wx_hi = sb("wx_hi", [P, C, DS], F32R)
        wx_lo = sb("wx_lo", [P, C, DS], F32R)
        wq = sb("wq", [P, C, 3 * D])
        wq_hi = sb("wq_hi", [P, C, 3 * D], F32R)
        wq_lo = sb("wq_lo", [P, C, 3 * D], F32R)
        wp = sb("wp", [P, C, D])
        a_rows = sb("a_rows", [P, 2, D])
        a_scratch = sb("a_scratch", [P, D])
        gbeta = sb("gbeta", [P, 1])
        bias_rows = sb("bias_rows", [P, D])
        bias_cast = sb("bias_cast", [P, 2, D], BF16)
        bias_rest = sb("bias_rest", [P, 2, D])
        bias_parts = sb("bias_parts", [3 * 32, D], BF16)
        bias_pick = sb("bias_pick", [3 * 32, P], BF16)
        gamma = sb("gamma", [P, D])
        lnb = sb("lnb", [P, D])
        ones = sb("ones", [P, HD])
        minus_half = sb("minus_half", [P, PAIR])
        minus_one = sb("minus_one", [P, PAIR])
        eps = sb("eps", [P, PAIR])
        beat = sb("beat", [P, 1])

        xs = sb("xs", [P, NG * GW])
        stats = [sb(f"stats{k}", [P, PAIR, 6]) for k in range(3)]
        moments = [sb(f"moments{k}", [P, PAIR, 2]) for k in range(3)]
        var_eps = [sb(f"var_eps{k}", [P, PAIR]) for k in range(3)]
        neg_mean = [sb(f"neg_mean{k}", [P, PAIR]) for k in range(3)]
        rstd = [sb(f"rstd{k}", [P, PAIR]) for k in range(3)]
        shift = [sb(f"shift{k}", [P, PAIR]) for k in range(3)]
        z0 = sb("z0", [P, GW])
        h0_hi = sb("h0_hi", [P, C, TOK], F32R)
        h0_lo = sb("h0_lo", [P, C, TOK], F32R)
        hw = two(sb, "hw", [P, PAIR, DS])
        s_sum = sb("s_sum", [P, PAIR, N])
        leaky = sb("leaky", [P, PAIR, N])
        masked = sb("masked", [P, PAIR, N])
        neg_max0 = sb("neg_max0", [P, PAIR])
        p0 = two(sb, "p0", [P, PAIR, N])
        sum0 = two(sb, "sum0", [P, PAIR])
        beta_sum0 = sb("beta_sum0", [P, PAIR])
        inv_sum0 = sb("inv_sum0", [P, PAIR])
        p0_t = sb("p0_t", [P, PAIR, N])
        exp_h = sb("exp_h", [P, PAIR, D])
        exp_m1 = sb("exp_m1", [P, PAIR, D])
        elu = sb("elu", [P, GW])
        x1 = sb("x1", [P, GW])
        z1 = sb("z1", [P, GW])
        h1_hi = two(sb, "h1_hi", [P, C, TOK], F32R)
        h1_lo = two(sb, "h1_lo", [P, C, TOK], F32R)
        qk = two(sb, "qk", [P, 4, C, TOK], F16)
        stack = two(sb, "stack", [STACK, 2, HC, C, TOK], F16)
        v = two(sb, "v", [P, PAIR, D])
        neg_max = sb("neg_max", [P, PAIR, H], BF16)
        p_t = two(sb, "p_t", [P, H, N])
        inv_sum = sb("inv_sum", [P, C, N])
        o_t = two(sb, "o_t", [P, C, N])
        y = sb("y", [P, PAIR, D])
        y_gamma = sb("y_gamma", [P, PAIR, D])
        res = sb("res", [P, GW])
        out_sb = two(sb, "out_sb", [P, GW])

        bk = [bank(f"bank{i}") for i in range(8)]

        const_loaded = sem("const_loaded")
        pool_const = sem("pool_const")
        dve_const = sem("dve_const")
        adj_t_done = sem("adj_t_done")
        ident_cleared = sem("ident_cleared")
        wx_ready_steps, bias_steps = sem("wx_ready_steps"), sem("bias_steps")
        wx_ready = sem("wx_ready")
        w_ready = sem("w_ready")
        x_loaded = two(sem, "x_loaded")
        stack_landed = two(sem, "stack_landed")
        out_stored = two(sem, "out_stored")
        tr0_done, hw_done, s2_done = sem("tr0_done"), sem("hw_done"), sem("s2_done")
        pt0_done, att0_done, tr1_done = sem("pt0_done"), sem("att0_done"), sem("tr1_done")
        q_done, k_done, v_done = sem("q_done"), sem("k_done"), sem("v_done")
        score_done = sem("score_done")
        score_t_done = sem("score_t_done")
        attend_done = sem("attend_done")
        proj_done = sem("proj_done")
        z0_ready, h0_hi_ready = sem("z0_ready"), sem("h0_hi_ready")
        hw_ready = sem("hw_ready")
        s_sum_ready, p0_ready, exp_ready = sem("s_sum_ready"), sem("p0_ready"), sem("exp_ready")
        leaky_ready = sem("leaky_ready")
        h1_hi_ready, q_hi_ready, k_hi_ready = sem("h1_hi_ready"), sem("q_hi_ready"), sem("k_hi_ready")
        v_ready = sem("v_ready")
        p_ready = sem("p_ready")
        y_ready = sem("y_ready")
        stats_ready = [sem(f"stats_ready{k}") for k in range(3)]
        moments_ready = [sem(f"moments_ready{k}") for k in range(3)]
        h0_lo_ready, sums0_ready, p0_t_ready = sem("h0_lo_ready"), sem("sums0_ready"), sem("p0_t_ready")
        exp_m1_ready, elu_ready, neg_max0_ready = sem("exp_m1_ready"), sem("elu_ready"), sem("neg_max0_ready")
        h1_lo_ready, q_lo_ready, k_lo_ready = sem("h1_lo_ready"), sem("q_lo_ready"), sem("k_lo_ready")
        max_ready = sem("max_ready")
        inv_ready = sem("inv_ready")
        o_ready = sem("o_ready")
        res_ready, out_ready = sem("res_ready"), sem("out_ready")
        eps_added = [sem(f"eps_added{k}") for k in range(3)]
        neg_mean_ready = [sem(f"neg_mean_ready{k}") for k in range(3)]
        rstd_ready = [sem(f"rstd_ready{k}") for k in range(3)]
        shift_ready = [sem(f"shift_ready{k}") for k in range(3)]
        masked_ready, x1_ready, z1_ready, y_gamma_ready = (
            sem("masked_ready"), sem("x1_ready"), sem("z1_ready"), sem("y_gamma_ready"))
        x1b_ready = sem("x1b_ready")

        x_dram = x.rearrange("b n d -> n b d")
        out_dram = out.rearrange("b n d -> n b d")

        def xs_of(g, b=None):
            if b is None:
                return xs[:, bass.ds(g * GW, GW)]
            return xs[:, bass.ds(g * GW + b * D, D)]

        def pairs(ap, w=D):
            return ap.rearrange("p (b w) -> p b w", w=w)

        CONSTS = 16 * 10

        def landed(g, slot):
            return 8 * (g - slot) + 16

        class Step:

            def __init__(self, t, low, high, parity):
                self.t, self.low, self.high, self.parity = t, low, high, parity

            def on(self, lag):
                return self.low - lag >= 0 and self.high - lag < NG

            def was_on(self, lag):
                return self.low - 1 - lag >= 0 and self.high - 1 - lag < NG

            def g(self, lag):
                return self.t - lag

            def later(self, lag):
                return self.low - lag >= 1

            def slot(self, lag):
                return (self.parity + lag) % 2

        def pipeline(eng, step):
            lead = LAST_LAG + 1 + (NG - LAST_LAG - 1) % 2
            for t in range(lead):
                step(Step(t, t, t, t % 2))
            with eng.Fori(0, (NG - lead) // 2) as k:
                t = lead + 2 * k
                step(Step(t, lead, NG - 2, lead % 2))
                step(Step(t + 1, lead + 1, NG - 1, (lead + 1) % 2))
            for t in range(NG, NG + LAST_LAG):
                step(Step(t, t, t, t % 2))

        block = ctx.enter_context(nc.Block())

        @block.sync
        def _(sp):
            def broadcast(ap, n):
                return ap.rearrange("(a n) -> a n", a=1).broadcast_to([P, n])

            sp.dma_start(adj_sb[:, :], adj).then_inc(const_loaded, 16)
            sp.dma_start(wx[:, :, 0:D], gat_w.rearrange("(c p) f -> p c f", p=P)).then_inc(const_loaded, 16)
            for k in range(2):
                a_k = gat_a[k * D:(k + 1) * D, :].rearrange("d a -> (d a)")
                sp.dma_start(a_rows[:, k, :], broadcast(a_k, D)).then_inc(const_loaded, 16)
            sp.dma_start(gbeta[:, :], broadcast(gat_beta, 1)).then_inc(const_loaded, 16)
            sp.dma_start(wq[:, :, :], w_qkv.rearrange("(c p) f -> p c f", p=P)).then_inc(const_loaded, 16)
            sp.dma_start(wp[:, :, :], w_proj.rearrange("(c p) f -> p c f", p=P)).then_inc(const_loaded, 16)
            for row, dst in ((b_proj, bias_rows), (ln_gamma, gamma), (ln_beta, lnb)):
                sp.dma_start(dst[:, :], broadcast(row, D)).then_inc(const_loaded, 16)

            for slot in range(2):
                sp.sem_inc(out_stored[slot], 16)

            def step(s):
                if s.on(LOAD):
                    g, slot = s.g(LOAD), s.slot(LOAD)
                    if s.low >= 2:
                        sp.wait_ge(x_loaded[slot], landed(g - 2, slot))
                    sp.dma_start(pairs(xs_of(g)), x_dram[:, bass.ds(g * PAIR, PAIR), :]).then_inc(x_loaded[slot], 16)
                if s.on(FINISH):
                    g, slot = s.g(FINISH), s.slot(FINISH)
                    sp.wait_ge(out_ready, g + 1)
                    sp.dma_start(out_dram[:, bass.ds(g * PAIR, PAIR), :],
                                 pairs(out_sb[slot][:, :])).then_inc(out_stored[slot], 16)
                if s.on(QK):
                    g, slot = s.g(QK), s.slot(QK)
                    sp.wait_ge(q_lo_ready, g + 1)
                    sp.wait_ge(k_lo_ready, g + 1)
                    if s.on(ATTEND):
                        sp.wait_ge(score_t_done, 4 * s.g(ATTEND) + 4)
                    for part, picks in enumerate((slice(0, 3, 2), slice(0, 4, 3), slice(1, 3, 1))):
                        for h in range(HC):
                            sp.dma_start(stack[slot][part * HD:(part + 1) * HD, :, h, :, :],
                                         qk[slot][h * HD:(h + 1) * HD, picks, :, :]).then_inc(stack_landed[slot], 16)

            pipeline(sp, step)
            for slot in range(2):
                sp.wait_ge(out_stored[slot], 16 * (NG // 2 + 1))

        @block.tensor
        def _(pe):
            def hi_lo(dst, lhs, rhs):
                n = 0
                for c in range(C):
                    for i, j in ((1, 0), (0, 1), (0, 0)):
                        mm = pe.matmul(dst, lhs(i, c), rhs(j, c), start=(n == 0), stop=(n == 3 * C - 1))
                        n += 1
                return mm

            def transposed(dst, src):
                for b in range(PAIR):
                    for c in range(C):
                        mm = pe.transpose(dst[:, c * TOK + b * N:c * TOK + (b + 1) * N],
                                          src[:, b * D + c * P:b * D + (c + 1) * P], ident[:, :])
                return mm

            def scores(g, slot, b, half, dst, flip, s):
                q, k = (1, 0) if flip else (0, 1)
                mask = mask_add_t if flip else mask_add
                d = dst[:, :].rearrange("p (h n) -> p h n", n=N)
                pe.matmul(d, ident_bf[:, :], mask[:, :].unsqueeze(1).broadcast_to([P, HC, N]),
                          start=True, stop=False, skip_group_check=True)
                for h in range(HC):
                    mm = pe.matmul(d[:, h, :], stack[slot][:, q, h, half, b * N:(b + 1) * N],
                                   stack[slot][:, k, h, half, b * N:(b + 1) * N],
                                   start=False, stop=(not flip), skip_group_check=True)
                if not flip:
                    mm.then_inc(score_done, 1)
                    return
                pe.wait_ge(max_ready, 4 * g + 2 * b + half + 1)
                for h in range(HC):
                    hh = half * HC + h
                    mm = pe.matmul(d[:, h, :], neg_max[:, b, hh:hh + 1].broadcast_to([P, N]), ident_bf[:, :],
                                   start=False, stop=True, skip_group_check=True)
                mm.then_inc(score_t_done, 1)

            def attend(g, slot, b, dst):
                for c in range(C):
                    for h in range(HC):
                        rows = slice(h * HD, (h + 1) * HD)
                        hh = c * HC + h
                        pe.matmul(dst[rows, c * N:(c + 1) * N], v[slot][:, b, hh * HD:(hh + 1) * HD],
                                  p_t[b][:, hh, :], start=True, stop=True)
                for c in range(C):
                    for h in range(HC):
                        rows = slice(h * HD, (h + 1) * HD)
                        mm = pe.matmul(dst[rows, (C + c) * N:(C + c + 1) * N], ones[:, :], p_t[b][:, c * HC + h, :],
                                       start=True, stop=True)
                mm.then_inc(attend_done, 1)

            pe.wait_ge(pool_const, 1)
            pe.wait_ge(const_loaded, CONSTS)
            pe.transpose(bk[0][:, 0:N], adj_sb[:, :], ident[:, :]).then_inc(adj_t_done, 1)
            pe.wait_ge(dve_const, 1)

            def step(s):
                t = s.t
                if s.on(GAT_IN):
                    g = s.g(GAT_IN)
                    if s.was_on(ATTEND):
                        pe.wait_ge(p_ready, 4 * (t - 1 - ATTEND) + 3)
                    elif s.later(GAT_IN):
                        pe.wait_ge(s_sum_ready, g)
                    pe.wait_ge(z0_ready, g + 1)
                    transposed(bk[1], z0).then_inc(tr0_done, 1)
                if s.on(QK):
                    g = s.g(QK)
                    if s.was_on(VALUES):
                        pe.wait_ge(v_ready, t - VALUES)
                    elif s.later(QK):
                        pe.wait_ge(q_lo_ready, g)
                    pe.wait_ge(z1_ready, g + 1)
                    transposed(bk[0], z1).then_inc(tr1_done, 1)
                if s.on(FINISH):
                    g = s.g(FINISH)
                    if s.later(FINISH):
                        pe.wait_ge(y_ready, g)
                        pe.wait_ge(res_ready, g)
                    pe.wait_ge(o_ready, 2 * g + 2)
                    for b in range(PAIR):
                        d = bk[7][:, b * D:(b + 1) * D]
                        pe.matmul(d, bias_pick[:, :], bias_parts[:, :], start=True, stop=False)
                        for c in range(C):
                            mm = pe.matmul(d, o_t[b][:, c, :], wp[:, c, :], start=False, stop=(c == C - 1))
                    mm.then_inc(proj_done, 1)
                if s.on(ATTEND):
                    g, slot = s.g(ATTEND), s.slot(ATTEND)
                    pe.wait_ge(stack_landed[slot], 12 * landed(g, slot))
                    if s.later(ATTEND):
                        pe.wait_ge(p_ready, 4 * g)
                        pe.wait_ge(max_ready, 4 * g)
                    scores(g, slot, 0, 0, bk[4], False, s)
                    scores(g, slot, 0, 1, bk[5], False, s)
                if s.on(GAT_OUT):
                    g, slot = s.g(GAT_OUT), s.slot(GAT_OUT)
                    if s.later(GAT_OUT):
                        pe.wait_ge(elu_ready, g)
                    pe.wait_ge(p0_ready, g + 1)
                    for b in range(PAIR):
                        mm = pe.transpose(bk[2][:, b * N:(b + 1) * N], p0[slot][:, b, :], ident[:, :])
                    mm.then_inc(pt0_done, 1)
                if s.on(GAT_IN):
                    g = s.g(GAT_IN)
                    pe.wait_ge(wx_ready, 1)
                    pe.wait_ge(h0_lo_ready, g + 1)
                    if s.was_on(QK):
                        pe.wait_ge(k_lo_ready, t - QK)
                    elif s.later(GAT_IN):
                        pe.wait_ge(hw_ready, 2 * g)
                    h0, w0 = (h0_hi, h0_lo), (wx_hi, wx_lo)
                    for b, d in enumerate((bk[1], bk[3])):
                        hi_lo(d[:, 0:DS], lambda i, c: h0[i][:, c, b * N:(b + 1) * N],
                              lambda j, c: w0[j][:, c, :]).then_inc(hw_done, 1)
                if s.on(ATTEND):
                    g, slot = s.g(ATTEND), s.slot(ATTEND)
                    if s.later(ATTEND):
                        pe.wait_ge(o_ready, 2 * g)
                    scores(g, slot, 0, 0, bk[6], True, s)
                    pe.wait_ge(max_ready, 4 * g + 2)
                    scores(g, slot, 0, 1, bk[5], True, s)
                if s.on(GAT_OUT):
                    g, slot = s.g(GAT_OUT), s.slot(GAT_OUT)
                    pe.wait_ge(p0_t_ready, g + 1)
                    for b in range(PAIR):
                        mm = pe.matmul(bk[2][:, b * D:(b + 1) * D], p0_t[:, b, :], hw[slot][:, b, 0:D],
                                       start=True, stop=True)
                    mm.then_inc(att0_done, 1)
                if s.on(QK):
                    g, slot = s.g(QK), s.slot(QK)
                    pe.wait_ge(w_ready, 1)
                    pe.wait_ge(h1_lo_ready, g + 1)
                    h1, w1 = (h1_hi[slot], h1_lo[slot]), (wq_hi, wq_lo)
                    for m in range(C):
                        mm = hi_lo(bk[0][:, m * TOK:(m + 1) * TOK], lambda i, c: w1[i][:, c, m * P:(m + 1) * P],
                                   lambda j, c: h1[j][:, c, :])
                    mm.then_inc(q_done, 1)
                if s.on(GAT_IN):
                    g, slot = s.g(GAT_IN), s.slot(GAT_IN)
                    pe.wait_ge(hw_ready, 2 * g + 2)
                    for b in range(PAIR):
                        mm = pe.transpose(bk[1][:, b * N:(b + 1) * N],
                                          hw[slot][:, b, D + 1:D + 2].broadcast_to([P, N]), ident[:, :])
                    mm.then_inc(s2_done, 1)
                if s.on(ATTEND):
                    g, slot = s.g(ATTEND), s.slot(ATTEND)
                    scores(g, slot, 1, 0, bk[4], False, s)
                    pe.wait_ge(p_ready, 4 * g + 2)
                    scores(g, slot, 1, 1, bk[5], False, s)
                    pe.wait_ge(v_ready, g + 1)
                    attend(g, slot, 0, bk[6])
                if s.on(QK):
                    g, slot = s.g(QK), s.slot(QK)
                    if s.on(GAT_IN):
                        pe.wait_ge(hw_ready, 2 * s.g(GAT_IN) + 2)
                    elif s.later(QK):
                        pe.wait_ge(k_lo_ready, g)
                    h1, w1 = (h1_hi[slot], h1_lo[slot]), (wq_hi, wq_lo)
                    for m in range(C):
                        mm = hi_lo(bk[3][:, m * TOK:(m + 1) * TOK],
                                   lambda i, c: w1[i][:, c, D + m * P:D + (m + 1) * P],
                                   lambda j, c: h1[j][:, c, :])
                    mm.then_inc(k_done, 1)
                if s.on(ATTEND):
                    g, slot = s.g(ATTEND), s.slot(ATTEND)
                    if s.on(GAT_IN):
                        pe.wait_ge(s_sum_ready, s.g(GAT_IN) + 1)
                    elif s.later(ATTEND):
                        pe.wait_ge(p_ready, 4 * g - 1)
                    scores(g, slot, 1, 0, bk[1], True, s)
                    scores(g, slot, 1, 1, bk[4], True, s)
                if s.on(VALUES):
                    g, slot = s.g(VALUES), s.slot(VALUES)
                    if s.on(QK):
                        pe.wait_ge(q_lo_ready, s.g(QK) + 1)
                    elif s.later(VALUES):
                        pe.wait_ge(v_ready, g)
                    h1, w1 = (h1_hi[slot], h1_lo[slot]), (wq_hi, wq_lo)
                    for b in range(PAIR):
                        mm = hi_lo(bk[0][:, b * D:(b + 1) * D], lambda i, c: h1[i][:, c, b * N:(b + 1) * N],
                                   lambda j, c: w1[j][:, c, 2 * D:3 * D])
                    mm.then_inc(v_done, 1)
                if s.on(ATTEND):
                    g, slot = s.g(ATTEND), s.slot(ATTEND)
                    pe.wait_ge(o_ready, 2 * g + 1)
                    pe.wait_ge(p_ready, 4 * g + 4)
                    attend(g, slot, 1, bk[6])

            pipeline(pe, step)

        @block.scalar
        def _(act):
            def exp_scores(s, b, half, src):
                g = s.g(ATTEND)
                act.wait_ge(score_t_done, 4 * g + 2 * b + half + 1)
                act.activation(p_t[b][:, half * HC:(half + 1) * HC, :], src[:, :].rearrange("p (h n) -> p h n", n=N),
                               ACT.Exp, scale=SCALE).then_inc(p_ready, 1)

            act.wait_ge(dve_const, 1)

            def step(s):
                if s.on(GAT_IN):
                    g = s.g(GAT_IN)
                    act.wait_ge(tr0_done, g + 1)
                    act.activation(h0_hi[:, :, :].rearrange("p c t -> p (c t)"), bk[1][:, :],
                                   ACT.Copy).then_inc(h0_hi_ready, 1)
                if s.on(QK):
                    g, slot = s.g(QK), s.slot(QK)
                    act.wait_ge(tr1_done, g + 1)
                    act.activation(h1_hi[slot][:, :, :].rearrange("p c t -> p (c t)"), bk[0][:, :],
                                   ACT.Relu).then_inc(h1_hi_ready, 1)
                if s.on(GAT_IN):
                    g, slot = s.g(GAT_IN), s.slot(GAT_IN)
                    for b, src in enumerate((bk[1], bk[3])):
                        act.wait_ge(hw_done, 2 * g + b + 1)
                        act.activation(hw[slot][:, b, :], src[:, 0:DS], ACT.Copy).then_inc(hw_ready, 1)
                if s.on(ATTEND):
                    exp_scores(s, 0, 0, bk[6])
                    exp_scores(s, 0, 1, bk[5])
                if s.on(GAT_OUT):
                    g = s.g(GAT_OUT)
                    act.wait_ge(att0_done, g + 1)
                    act.wait_ge(sums0_ready, g + 1)
                    for b in range(PAIR):
                        ins = act.activation(exp_h[:, b, :], bk[2][:, b * D:(b + 1) * D], ACT.Exp,
                                             scale=inv_sum0[:, b:b + 1])
                    ins.then_inc(exp_ready, 1)
                if s.on(QK):
                    g, slot = s.g(QK), s.slot(QK)
                    act.wait_ge(q_done, g + 1)
                    act.activation(qk[slot][:, 0, :, :].rearrange("p c t -> p (c t)"), bk[0][:, :],
                                   ACT.Copy).then_inc(q_hi_ready, 1)
                if s.on(GAT_IN):
                    g, slot = s.g(GAT_IN), s.slot(GAT_IN)
                    act.wait_ge(s2_done, g + 1)
                    for b in range(PAIR):
                        ins = act.activation(s_sum[:, b, :], bk[1][:, b * N:(b + 1) * N], ACT.Identity,
                                             bias=hw[slot][:, b, D:D + 1])
                    ins.then_inc(s_sum_ready, 1)
                if s.on(FINISH):
                    g = s.g(FINISH)
                    act.wait_ge(shift_ready[2], g + 1)
                    act.wait_ge(res_ready, g + 1)
                    for b in range(PAIR):
                        ins = act.activation(y[:, b, :], bk[7][:, b * D:(b + 1) * D], ACT.Identity,
                                             scale=rstd[2][:, b:b + 1], bias=shift[2][:, b:b + 1])
                    ins.then_inc(y_ready, 1)
                if s.on(NORM0):
                    g = s.g(NORM0)
                    act.wait_ge(shift_ready[0], g + 1)
                    if s.later(NORM0):
                        act.wait_ge(tr0_done, g)
                    for b in range(PAIR):
                        ins = act.activation(z0[:, b * D:(b + 1) * D], xs_of(g, b), ACT.Relu,
                                             scale=rstd[0][:, b:b + 1], bias=shift[0][:, b:b + 1])
                    ins.then_inc(z0_ready, 1)
                if s.on(QK):
                    g, slot = s.g(QK), s.slot(QK)
                    act.wait_ge(k_done, g + 1)
                    act.activation(qk[slot][:, 2, :, :].rearrange("p c t -> p (c t)"), bk[3][:, :],
                                   ACT.Copy).then_inc(k_hi_ready, 1)
                if s.on(GAT_IN):
                    g, slot = s.g(GAT_IN), s.slot(GAT_IN)
                    act.wait_ge(neg_max0_ready, g + 1)
                    for b in range(PAIR):
                        ins = act.activation(p0[slot][:, b, :], masked[:, b, :], ACT.Exp,
                                             bias=neg_max0[:, b:b + 1], accum_out=sum0[slot][:, b:b + 1])
                    ins.then_inc(p0_ready, 1)
                if s.on(ATTEND):
                    exp_scores(s, 1, 0, bk[1])
                    exp_scores(s, 1, 1, bk[4])
                if s.on(VALUES):
                    g, slot = s.g(VALUES), s.slot(VALUES)
                    act.wait_ge(v_done, g + 1)
                    act.activation(v[slot][:, :, :].rearrange("p b d -> p (b d)"), bk[0][:, :],
                                   ACT.Copy).then_inc(v_ready, 1)

            pipeline(act, step)

        @block.vector
        def _(dve):
            dve.wait_ge(const_loaded, CONSTS)
            n = 0
            for k in range(2):
                for c in range(C):
                    if n:
                        dve.wait_ge(wx_ready_steps, n)
                    dve.tensor_tensor_reduce(a_scratch[:, :], wx[:, c, 0:D], a_rows[:, k, :], 1.0, 0.0, ALU.mult,
                                             ALU.add, wx[:, c, D + k:D + k + 1]).then_inc(wx_ready_steps, 1)
                    n += 1
            dve.wait_ge(wx_ready_steps, n)
            dve.tensor_copy(wx_hi[:, :, :], wx[:, :, :]).then_inc(wx_ready_steps, 1)
            dve.wait_ge(wx_ready_steps, n + 1)
            dve.tensor_tensor(wx_lo[:, :, :], wx[:, :, :], wx_hi[:, :, :].bitcast(F32),
                              ALU.subtract).then_inc(wx_ready, 1)
            dve.tensor_scalar(mask_add[:, :], adj_sb[:, :], 0.0, MASKED, ALU.is_equal, ALU.mult)
            dve.wait_ge(adj_t_done, 1)
            dve.tensor_scalar(mask_add_t[:, :], bk[0][:, 0:N], 0.0, MASKED, ALU.is_equal, ALU.mult)
            dve.memset(bias_pick[:, :], 1.0 / 32)
            dve.memset(ones[:, :], 1.0)
            dve.tensor_copy(bias_parts[0:32, :], bias_rows[0:32, :])
            dve.tensor_copy(bias_cast[:, 0, :], bias_rows[:, :]).then_inc(bias_steps, 1)
            dve.wait_ge(bias_steps, 1)
            dve.tensor_tensor(bias_rest[:, 0, :], bias_rows[:, :], bias_cast[:, 0, :],
                              ALU.subtract).then_inc(bias_steps, 1)
            dve.wait_ge(bias_steps, 2)
            dve.tensor_copy(bias_parts[32:64, :], bias_rest[32:64, 0, :])
            dve.tensor_copy(bias_cast[:, 1, :], bias_rest[:, 0, :]).then_inc(bias_steps, 1)
            dve.wait_ge(bias_steps, 3)
            dve.tensor_tensor(bias_rest[:, 1, :], bias_rest[:, 0, :], bias_cast[:, 1, :],
                              ALU.subtract).then_inc(bias_steps, 1)
            dve.wait_ge(bias_steps, 4)
            dve.tensor_copy(bias_parts[64:96, :], bias_rest[64:96, 1, :]).then_inc(dve_const, 1)

            def split_w():
                dve.tensor_copy(wq_hi[:, :, :], wq[:, :, :]).then_inc(wx_ready_steps, 1)
                dve.wait_ge(wx_ready_steps, n + 2)
                dve.tensor_tensor(wq_lo[:, :, :], wq[:, :, :], wq_hi[:, :, :].bitcast(F32),
                                  ALU.subtract).then_inc(w_ready, 1)

            def layer_stats(k, g, src):
                for b in range(PAIR):
                    ins = dve.bn_stats(stats[k][:, b, :], src(b))
                ins.then_inc(stats_ready[k], 1)
                dve.wait_ge(stats_ready[k], g + 1)
                dve.memset(beat[:, :], 0.0)
                for b in range(PAIR):
                    ins = dve.bn_aggr(moments[k][:, b, :], stats[k][:, b, :])
                ins.then_inc(moments_ready[k], 1)

            def maxima(s, b, half, src):
                g = s.g(ATTEND)
                dve.wait_ge(score_done, 4 * g + 2 * b + half + 1)
                dve.tensor_reduce(neg_max[:, b, half * HC:(half + 1) * HC],
                                  src[:, :].rearrange("p (h n) -> p h n", n=N), AX_X, ALU.max,
                                  negate=True).then_inc(max_ready, 1)

            def normalize(s, b):
                g = s.g(ATTEND)
                dve.wait_ge(attend_done, 2 * g + b + 1)
                dve.reciprocal(inv_sum[:, :, :].rearrange("p c n -> p (c n)"),
                               bk[6][:, C * N:2 * C * N]).then_inc(inv_ready, 1)
                dve.wait_ge(inv_ready, 2 * g + b + 1)
                dve.tensor_tensor(o_t[b][:, :, :].rearrange("p c n -> p (c n)"), bk[6][:, 0:C * N],
                                  inv_sum[:, :, :].rearrange("p c n -> p (c n)"), ALU.mult).then_inc(o_ready, 1)

            def step(s):
                if s.low == 0 and s.high == 0:
                    split_w()
                if s.on(GAT_IN):
                    g = s.g(GAT_IN)
                    dve.wait_ge(h0_hi_ready, g + 1)
                    dve.tensor_tensor(h0_lo[:, :, :].rearrange("p c t -> p (c t)"), bk[1][:, :],
                                      h0_hi[:, :, :].bitcast(F32).rearrange("p c t -> p (c t)"),
                                      ALU.subtract).then_inc(h0_lo_ready, 1)
                if s.on(QK):
                    g, slot = s.g(QK), s.slot(QK)
                    dve.wait_ge(h1_hi_ready, g + 1)
                    dve.scalar_tensor_tensor(out=h1_lo[slot][:, :, :].rearrange("p c t -> p (c t)"), in0=bk[0][:, :],
                                             scalar=0.0,
                                             in1=h1_hi[slot][:, :, :].bitcast(F32).rearrange("p c t -> p (c t)"),
                                             op0=ALU.max, op1=ALU.subtract).then_inc(h1_lo_ready, 1)
                if s.on(GAT_OUT):
                    g, slot = s.g(GAT_OUT), s.slot(GAT_OUT)
                    dve.wait_ge(p0_ready, g + 1)
                    dve.tensor_scalar(beta_sum0[:, :], sum0[slot][:, :], gbeta[:, 0:1], None, ALU.mult)
                    dve.reciprocal(inv_sum0[:, :], sum0[slot][:, :]).then_inc(sums0_ready, 1)
                if s.on(ATTEND):
                    maxima(s, 0, 0, bk[4])
                    maxima(s, 0, 1, bk[5])
                if s.on(GAT_OUT):
                    g = s.g(GAT_OUT)
                    dve.wait_ge(pt0_done, g + 1)
                    dve.wait_ge(sums0_ready, g + 1)
                    for b in range(PAIR):
                        ins = dve.scalar_tensor_tensor(out=p0_t[:, b, :], in0=ident[:, :],
                                                       scalar=beta_sum0[:, b:b + 1], in1=bk[2][:, b * N:(b + 1) * N],
                                                       op0=ALU.mult, op1=ALU.add)
                    ins.then_inc(p0_t_ready, 1)
                if s.on(FINISH):
                    g = s.g(FINISH)
                    dve.wait_ge(proj_done, g + 1)
                    layer_stats(2, g, lambda b: bk[7][:, b * D:(b + 1) * D])
                    dve.wait_ge(x1b_ready, g + 1)
                    dve.tensor_tensor(res[:, :], bk[7][:, :], xs_of(g), ALU.add).then_inc(res_ready, 1)
                if s.on(NORM0):
                    g, slot = s.g(NORM0), s.slot(NORM0)
                    dve.wait_ge(x_loaded[slot], landed(g, slot))
                    layer_stats(0, g, lambda b: xs_of(g, b))
                if s.on(GAT_OUT):
                    g = s.g(GAT_OUT)
                    dve.wait_ge(exp_ready, g + 1)
                    dve.tensor_scalar(exp_m1[:, :, :], exp_h[:, :, :], 1.0, 1.0, ALU.min,
                                      ALU.subtract).then_inc(exp_m1_ready, 1)
                    dve.wait_ge(exp_m1_ready, g + 1)
                    for b in range(PAIR):
                        ins = dve.scalar_tensor_tensor(out=elu[:, b * D:(b + 1) * D], in0=bk[2][:, b * D:(b + 1) * D],
                                                       scalar=inv_sum0[:, b:b + 1], in1=exp_m1[:, b, :],
                                                       op0=ALU.mult, op1=ALU.max)
                    ins.then_inc(elu_ready, 1)
                if s.on(QK):
                    g, slot = s.g(QK), s.slot(QK)
                    dve.wait_ge(q_hi_ready, g + 1)
                    dve.tensor_tensor(qk[slot][:, 1, :, :].rearrange("p c t -> p (c t)"), bk[0][:, :],
                                      qk[slot][:, 0, :, :].rearrange("p c t -> p (c t)"),
                                      ALU.subtract).then_inc(q_lo_ready, 1)
                if s.on(GAT_IN):
                    g = s.g(GAT_IN)
                    dve.wait_ge(s_sum_ready, g + 1)
                    dve.scalar_tensor_tensor(out=leaky[:, :, :], in0=s_sum[:, :, :], scalar=LEAKY_SLOPE,
                                             in1=s_sum[:, :, :], op0=ALU.mult, op1=ALU.max).then_inc(leaky_ready, 1)
                if s.on(ATTEND):
                    maxima(s, 1, 0, bk[4])
                    maxima(s, 1, 1, bk[5])
                    normalize(s, 0)
                if s.on(FINISH):
                    g, slot = s.g(FINISH), s.slot(FINISH)
                    dve.wait_ge(y_gamma_ready, g + 1)
                    dve.wait_ge(res_ready, g + 1)
                    dve.wait_ge(out_stored[slot], landed(g, slot))
                    dve.tensor_tensor(out_sb[slot][:, :], y_gamma[:, :, :].rearrange("p b d -> p (b d)"), res[:, :],
                                      ALU.add).then_inc(out_ready, 1)
                if s.on(GAT_IN):
                    g = s.g(GAT_IN)
                    dve.wait_ge(masked_ready, g + 1)
                    dve.tensor_reduce(neg_max0[:, :], masked[:, :, :], AX_X, ALU.max,
                                      negate=True).then_inc(neg_max0_ready, 1)
                if s.on(GAT_OUT):
                    g = s.g(GAT_OUT)
                    dve.wait_ge(x1_ready, g + 1)
                    layer_stats(1, g, lambda b: x1[:, b * D:(b + 1) * D])
                if s.on(QK):
                    g, slot = s.g(QK), s.slot(QK)
                    dve.wait_ge(k_hi_ready, g + 1)
                    dve.tensor_tensor(qk[slot][:, 3, :, :].rearrange("p c t -> p (c t)"), bk[3][:, :],
                                      qk[slot][:, 2, :, :].rearrange("p c t -> p (c t)"),
                                      ALU.subtract).then_inc(k_lo_ready, 1)
                if s.on(ATTEND):
                    normalize(s, 1)

            pipeline(dve, step)

        @block.gpsimd
        def _(pool):
            pool.memset(minus_half[:, :], -0.5)
            pool.memset(minus_one[:, :], -1.0)
            pool.memset(eps[:, :], LN_EPS)
            pool.memset(ident[:, :], 0.0).then_inc(ident_cleared, 1)
            pool.wait_ge(ident_cleared, 1)
            pool.affine_select(out=ident[:, :], in_=ident[:, :], compare_op=ALU.not_equal, fill=1.0, base=0,
                               pattern=[[-1, P]], channel_multiplier=1).then_inc(pool_const, 1)
            pool.wait_ge(pool_const, 1)
            pool.tensor_copy(ident_bf[:, :], ident[:, :]).then_inc(pool_const, 1)
            pool.wait_ge(pool_const, 2)

            def norm(k, g):
                pool.wait_ge(moments_ready[k], g + 1)
                pool.tensor_tensor(var_eps[k][:, :], moments[k][:, :, 1], eps[:, :],
                                   ALU.add).then_inc(eps_added[k], 1)
                pool.tensor_tensor(neg_mean[k][:, :], moments[k][:, :, 0], minus_one[:, :],
                                   ALU.mult).then_inc(neg_mean_ready[k], 1)
                pool.wait_ge(eps_added[k], g + 1)
                pool.tensor_tensor(rstd[k][:, :], var_eps[k][:, :], minus_half[:, :],
                                   ALU.pow).then_inc(rstd_ready[k], 1)
                pool.wait_ge(rstd_ready[k], g + 1)
                pool.wait_ge(neg_mean_ready[k], g + 1)
                pool.tensor_tensor(shift[k][:, :], neg_mean[k][:, :], rstd[k][:, :],
                                   ALU.mult).then_inc(shift_ready[k], 1)

            def step(s):
                if s.on(FINISH):
                    norm(2, s.g(FINISH))
                if s.on(NORM0):
                    norm(0, s.g(NORM0))
                if s.on(GAT_OUT):
                    g = s.g(GAT_OUT)
                    pool.wait_ge(elu_ready, g + 1)
                    pool.tensor_tensor(x1[:, :], elu[:, :], xs_of(g), ALU.add).then_inc(x1_ready, 1)
                if s.on(GAT_IN):
                    g = s.g(GAT_IN)
                    pool.wait_ge(leaky_ready, g + 1)
                    pool.tensor_tensor(masked[:, :, :], leaky[:, :, :],
                                       adj_sb[:, :].unsqueeze(1).broadcast_to([P, PAIR, N]),
                                       ALU.mult).then_inc(masked_ready, 1)
                if s.on(FINISH):
                    g = s.g(FINISH)
                    pool.wait_ge(y_ready, g + 1)
                    pool.tensor_tensor(y_gamma[:, :, :], y[:, :, :],
                                       gamma[:, :].unsqueeze(1).broadcast_to([P, PAIR, D]),
                                       ALU.mult).then_inc(y_gamma_ready, 1)
                if s.on(GAT_OUT):
                    g = s.g(GAT_OUT)
                    norm(1, g)
                    for b in range(PAIR):
                        ins = pool.tensor_scalar(z1[:, b * D:(b + 1) * D], x1[:, b * D:(b + 1) * D],
                                                 neg_mean[1][:, b:b + 1], rstd[1][:, b:b + 1], ALU.add, ALU.mult)
                    ins.then_inc(z1_ready, 1)
                    pool.tensor_tensor(pairs(xs_of(g)), pairs(x1[:, :]),
                                       lnb[:, :].unsqueeze(1).broadcast_to([P, PAIR, D]),
                                       ALU.add).then_inc(x1b_ready, 1)

            pool.wait_ge(const_loaded, CONSTS)
            pipeline(pool, step)


_INS = ['x', 'adj', 'L0_gnn_W', 'L0_gnn_a', 'L0_gnn_beta', 'L1_gnn_w_qkv', 'L1_gnn_w_proj', 'L1_gnn_b_proj',
        'L1_gnn_ln_gamma', 'L1_gnn_ln_beta']


def kernel(**inputs):
    import numpy as _np
    import concourse.bacc as _bacc
    from concourse import mybir as _mybir
    from concourse.bass_utils import run_bass_kernel_spmd as _run

    nc = _bacc.Bacc("TRN2", target_bir_lowering=False, num_devices=1)
    arrays, args = {}, []
    for name in _INS:
        a = _np.ascontiguousarray(inputs[name])
        arrays[f"in_{name}_dram"] = a
        args.append(nc.dram_tensor(f"in_{name}_dram", a.shape, _mybir.dt.from_np(a.dtype), kind="ExternalInput").ap())
    shape = inputs['x'].shape
    args.append(nc.dram_tensor("out_0_dram", shape, _mybir.dt.float32, kind="ExternalOutput").ap())
    gat_transformer(nc, *args)
    r = _run(nc, [arrays], core_ids=[0])
    return r.results[0]["out_0_dram"]
```

```python
from contextlib import ExitStack

import concourse.bass as bass
from concourse import mybir

ALU = mybir.AluOpType
ACT = mybir.ActivationFunctionType
AX_X = mybir.AxisListType.X
F32 = mybir.dt.float32
F32R = mybir.dt.float32r
F16 = mybir.dt.float16
BF16 = mybir.dt.bfloat16

P = 128
LN_EPS = 1e-5
LEAKY_SLOPE = 0.2
MASKED = -1e30

LAST_LAG = 7


def gat_transformer(nc, x, adj, gat_w, gat_a, gat_beta, w_qkv, w_proj, b_proj, ln_gamma, ln_beta, out):
    B, N, D = x.shape
    C = D // P
    H = 8
    HD = D // H
    HC = P // HD
    SCALE = float(HD) ** -0.5
    PAIR = 2
    NG = B // PAIR
    TOK = PAIR * N
    GW = PAIR * D
    DS = D + 2
    STACK = 3 * HD
    assert N == P and C == 2 and NG > LAST_LAG

    with ExitStack() as ctx:
        def sb(name, shape, dt=F32):
            return ctx.enter_context(nc.sbuf_tensor(name, shape, dt))

        def bank(name):
            return ctx.enter_context(nc.psum_tensor(name, [P, 512], F32))

        def sem(name):
            return ctx.enter_context(nc.semaphore(name))

        def two(make, name, *args):
            return [make(f"{name}{i}", *args) for i in range(2)]

        ident = sb("ident", [P, P])
        ident_bf = sb("ident_bf", [P, P], BF16)
        adj_sb = sb("adj_sb", [P, N])
        mask_add = sb("mask_add", [P, N], BF16)
        wx = sb("wx", [P, C, DS])
        wx_hi = sb("wx_hi", [P, C, DS], F32R)
        wx_lo = sb("wx_lo", [P, C, DS], F32R)
        wq = sb("wq", [P, C, 3 * D])
        wq_hi = sb("wq_hi", [P, C, 3 * D], F32R)
        wq_lo = sb("wq_lo", [P, C, 3 * D], F32R)
        wp = sb("wp", [P, C, D])
        a_rows = sb("a_rows", [P, 2, D])
        a_scratch = sb("a_scratch", [P, D])
        gbeta = sb("gbeta", [P, 1])
        bias_rows = sb("bias_rows", [P, D])
        bias_cast = sb("bias_cast", [P, 2, D], BF16)
        bias_rest = sb("bias_rest", [P, 2, D])
        bias_parts = sb("bias_parts", [3 * 32, D], BF16)
        bias_pick = sb("bias_pick", [3 * 32, P], BF16)
        gamma = sb("gamma", [P, D])
        lnb = sb("lnb", [P, D])
        minus_half = sb("minus_half", [P, PAIR])
        minus_one = sb("minus_one", [P, PAIR])
        eps = sb("eps", [P, PAIR])
        beat, pool_beat = sb("beat", [P, 1]), sb("pool_beat", [P, PAIR])

        xs = sb("xs", [P, NG * GW])
        stats = [sb(f"stats{k}", [P, PAIR, 6]) for k in range(3)]
        moments = [sb(f"moments{k}", [P, PAIR, 2]) for k in range(3)]
        var_eps = [sb(f"var_eps{k}", [P, PAIR]) for k in range(3)]
        neg_mean = [sb(f"neg_mean{k}", [P, PAIR]) for k in range(3)]
        rstd = [sb(f"rstd{k}", [P, PAIR]) for k in range(3)]
        shift = [sb(f"shift{k}", [P, PAIR]) for k in range(3)]
        centred = sb("centred", [P, GW])
        z0 = sb("z0", [P, GW])
        h0_hi = sb("h0_hi", [P, C, TOK], F32R)
        h0_lo = sb("h0_lo", [P, C, TOK], F32R)
        hw = two(sb, "hw", [P, PAIR, DS])
        s_sum = sb("s_sum", [P, PAIR, N])
        leaky = sb("leaky", [P, PAIR, N])
        masked = sb("masked", [P, PAIR, N])
        neg_max0 = sb("neg_max0", [P, PAIR])
        p0 = sb("p0", [P, PAIR, N])
        sum0 = sb("sum0", [P, PAIR])
        beta_sum0 = sb("beta_sum0", [P, PAIR])
        inv_sum0 = sb("inv_sum0", [P, PAIR])
        p0_t = sb("p0_t", [P, PAIR, N])
        exp_h = sb("exp_h", [P, PAIR, D])
        exp_m1 = sb("exp_m1", [P, PAIR, D])
        elu = sb("elu", [P, GW])
        x1 = sb("x1", [P, GW])
        z1 = sb("z1", [P, GW])
        h1_hi = two(sb, "h1_hi", [P, C, TOK], F32R)
        h1_lo = two(sb, "h1_lo", [P, C, TOK], F32R)
        qk = two(sb, "qk", [P, 4, C, TOK], F16)
        stack = two(sb, "stack", [STACK, 2, HC, C, TOK], F16)
        v = two(sb, "v", [P, PAIR, D])
        neg_max = sb("neg_max", [P, PAIR, H])
        p = sb("p", [P, PAIR, H, N])
        p_t = sb("p_t", [P, PAIR, H, N])
        sums = sb("sums", [P, PAIR, H])
        inv_sum = sb("inv_sum", [P, PAIR * H])
        inv_rep = sb("inv_rep", [P, PAIR * H, HD])
        inv_t = sb("inv_t", [P, PAIR * C * N])
        o_t = sb("o_t", [P, PAIR * C * N])
        y = sb("y", [P, PAIR, D])
        y_gamma = sb("y_gamma", [P, PAIR, D])
        res = sb("res", [P, GW])
        out_sb = two(sb, "out_sb", [P, GW])

        bk = [bank(f"bank{i}") for i in range(8)]

        early_loaded, late_loaded = sem("early_loaded"), sem("late_loaded")
        pool_const = sem("pool_const")
        ident_cleared = sem("ident_cleared")
        w_steps, bias_steps = sem("w_steps"), sem("bias_steps")
        wx_ready, w_hi_ready, w_ready, bias_ready = sem("wx_ready"), sem("w_hi_ready"), sem("w_ready"), sem("bias_ready")
        mask_ready = sem("mask_ready")
        x_loaded = two(sem, "x_loaded")
        stack_landed = two(sem, "stack_landed")
        out_stored = two(sem, "out_stored")
        stats_ready = [sem(f"stats_ready{k}") for k in range(3)]
        moments_ready = [sem(f"moments_ready{k}") for k in range(3)]
        eps_added = [sem(f"eps_added{k}") for k in range(3)]
        neg_mean_ready = [sem(f"neg_mean_ready{k}") for k in range(3)]
        rstd_ready = [sem(f"rstd_ready{k}") for k in range(3)]
        shift_ready = [sem(f"shift_ready{k}") for k in range(3)]
        recip_done, centred_ready = sem("recip_done"), sem("centred_ready")
        z0_ready = sem("z0_ready")
        z0_turned = sem("z0_turned")
        h0_hi_ready = sem("h0_hi_ready")
        h0_lo_ready = sem("h0_lo_ready")
        hw0_done = sem("hw0_done")
        hw1_done = sem("hw1_done")
        hw0_ready = sem("hw0_ready")
        hw1_ready = sem("hw1_ready")
        s2_turned = sem("s2_turned")
        s_sum_ready = sem("s_sum_ready")
        leaky_ready = sem("leaky_ready")
        masked_ready = sem("masked_ready")
        max0_ready = sem("max0_ready")
        p0_ready = sem("p0_ready")
        inv0_ready = sem("inv0_ready")
        p0_turned = sem("p0_turned")
        p0_t_ready = sem("p0_t_ready")
        att0_done = sem("att0_done")
        exp_ready = sem("exp_ready")
        exp_m1_ready = sem("exp_m1_ready")
        elu_ready = sem("elu_ready")
        x1_ready = sem("x1_ready")
        z1_ready = sem("z1_ready")
        x1b_ready = sem("x1b_ready")
        z1_turned = sem("z1_turned")
        h1_hi_ready = sem("h1_hi_ready")
        h1_lo_ready = sem("h1_lo_ready")
        q_done = sem("q_done")
        k_done = sem("k_done")
        v_done = sem("v_done")
        q_hi_ready = sem("q_hi_ready")
        q_lo_ready = sem("q_lo_ready")
        k_hi_ready = sem("k_hi_ready")
        k_lo_ready = sem("k_lo_ready")
        v_ready = sem("v_ready")
        scores00_done = sem("scores00_done")
        max00_ready = sem("max00_ready")
        p00_ready = sem("p00_ready")
        p00_turned = sem("p00_turned")
        p_t00_ready = sem("p_t00_ready")
        scores01_done = sem("scores01_done")
        max01_ready = sem("max01_ready")
        p01_ready = sem("p01_ready")
        p01_turned = sem("p01_turned")
        p_t01_ready = sem("p_t01_ready")
        scores10_done = sem("scores10_done")
        max10_ready = sem("max10_ready")
        p10_ready = sem("p10_ready")
        p10_turned = sem("p10_turned")
        p_t10_ready = sem("p_t10_ready")
        scores11_done = sem("scores11_done")
        max11_ready = sem("max11_ready")
        p11_ready = sem("p11_ready")
        p11_turned = sem("p11_turned")
        p_t11_ready = sem("p_t11_ready")
        inv_ready = sem("inv_ready")
        inv_turned = sem("inv_turned")
        inv_t_ready = sem("inv_t_ready")
        av_done = sem("av_done")
        o_ready = sem("o_ready")
        proj_done = sem("proj_done")
        res_ready = sem("res_ready")
        y_ready = sem("y_ready")
        y_gamma_ready = sem("y_gamma_ready")
        out_ready = sem("out_ready")

        x_dram = x.rearrange("b n d -> n b d")
        out_dram = out.rearrange("b n d -> n b d")

        def xs_of(g, b=None):
            if b is None:
                return xs[:, bass.ds(g * GW, GW)]
            return xs[:, bass.ds(g * GW + b * D, D)]

        def pairs(ap, w=D):
            return ap.rearrange("p (b w) -> p b w", w=w)

        EARLY, LATE = 16 * 5, 16 * 5

        def flat4(ap):
            return ap.rearrange("p c t -> p (c t)")

        def flat(tile):
            return flat4(tile[:, :, :])

        def turned_p(b, half):
            return p_t[:, b, half * HC:(half + 1) * HC, :].rearrange("p h n -> p (h n)")

        def landed(g, slot):
            return 8 * (g - slot) + 16

        class Step:

            def __init__(self, t, low, high, parity):
                self.t, self.low, self.high, self.parity = t, low, high, parity
                self.edge = low == high

            def on(self, lag):
                return self.low - lag >= 0 and self.high - lag < NG

            def was_on(self, lag):
                return self.low - 1 - lag >= 0 and self.high - 1 - lag < NG

            def first(self, lag):
                return self.low == self.high == lag

            def from_group(self, n, lag):
                return self.low - lag >= n

            def slot(self, lag):
                return (self.parity + lag) % 2

        def pipeline(eng, step):
            lead = LAST_LAG + 1 + (NG - LAST_LAG - 1) % 2
            for t in range(lead):
                step(Step(t, t, t, t % 2))
            with eng.Fori(0, (NG - lead) // 2) as k:
                t = lead + 2 * k
                step(Step(t, lead, NG - 2, lead % 2))
                step(Step(t + 1, lead + 1, NG - 1, (lead + 1) % 2))
            for t in range(NG, NG + LAST_LAG):
                step(Step(t, t, t, t % 2))

        block = ctx.enter_context(nc.Block())

        @block.sync
        def _(sp):
            def broadcast(ap, n):
                return ap.rearrange("(a n) -> a n", a=1).broadcast_to([P, n])

            sp.dma_start(pairs(xs_of(0)), x_dram[:, 0:PAIR, :]).then_inc(x_loaded[0], 16)
            sp.dma_start(wx[:, :, 0:D], gat_w.rearrange("(c p) f -> p c f", p=P)).then_inc(early_loaded, 16)
            for k in range(2):
                a_k = gat_a[k * D:(k + 1) * D, :].rearrange("d a -> (d a)")
                sp.dma_start(a_rows[:, k, :], broadcast(a_k, D)).then_inc(early_loaded, 16)
            sp.dma_start(adj_sb[:, :], adj).then_inc(early_loaded, 16)
            sp.dma_start(gbeta[:, :], broadcast(gat_beta, 1)).then_inc(early_loaded, 16)

            def load_late():
                sp.dma_start(wq[:, :, :], w_qkv.rearrange("(c p) f -> p c f", p=P)).then_inc(late_loaded, 16)
                sp.dma_start(wp[:, :, :], w_proj.rearrange("(c p) f -> p c f", p=P)).then_inc(late_loaded, 16)
                for row, dst in ((b_proj, bias_rows), (ln_gamma, gamma), (ln_beta, lnb)):
                    sp.dma_start(dst[:, :], broadcast(row, D)).then_inc(late_loaded, 16)

            for slot in range(2):
                sp.sem_inc(out_stored[slot], 16)

            def step(s):
                t = s.t
                if s.on(0):
                    g, slot = t, s.slot(0)
                    if s.low >= 2:
                        sp.wait_ge(x_loaded[slot], landed(g - 2, slot))
                    if not s.first(0):
                        sp.dma_start(pairs(xs_of(g)), x_dram[:, bass.ds(g * PAIR, PAIR), :]).then_inc(x_loaded[slot], 16)
                if s.on(4):
                    g, slot = t - 4, s.slot(4)
                    sp.wait_ge(q_lo_ready, g + 1)
                    sp.wait_ge(k_lo_ready, g + 1)
                    for part, picks in enumerate((slice(0, 3, 2), slice(0, 4, 3), slice(1, 3, 1))):
                        for h in range(HC):
                            sp.dma_start(stack[slot][part * HD:(part + 1) * HD, :, h, :, :],
                                         qk[slot][h * HD:(h + 1) * HD, picks, :, :]).then_inc(stack_landed[slot], 16)
                if s.on(7):
                    g, slot = t - 7, s.slot(7)
                    sp.wait_ge(out_ready, g + 1)
                    sp.dma_start(out_dram[:, bass.ds(g * PAIR, PAIR), :], pairs(out_sb[slot][:, :])).then_inc(out_stored[slot], 16)
                if s.first(0):
                    load_late()

            pipeline(sp, step)
            for slot in range(2):
                sp.wait_ge(out_stored[slot], 16 * (NG // 2 + 1))

        @block.tensor
        def _(pe):
            def hi_lo(dst, lhs, rhs):
                n = 0
                for c in range(C):
                    for i, j in ((1, 0), (0, 1), (0, 0)):
                        mm = pe.matmul(dst, lhs(i, c), rhs(j, c), start=(n == 0), stop=(n == 3 * C - 1))
                        n += 1
                return mm

            def transposed(dst, src):
                for b in range(PAIR):
                    for c in range(C):
                        mm = pe.transpose(dst[:, c * TOK + b * N:c * TOK + (b + 1) * N],
                                          src[:, b * D + c * P:b * D + (c + 1) * P], ident[:, :])
                return mm

            def gat_product(dst, b):
                h0, w0 = (h0_hi, h0_lo), (wx_hi, wx_lo)
                return hi_lo(dst[:, 0:DS], lambda i, c: h0[i][:, c, b * N:(b + 1) * N], lambda j, c: w0[j][:, c, :])

            def qk_product(dst, slot, which):
                h1, w1 = (h1_hi[slot], h1_lo[slot]), (wq_hi, wq_lo)
                for m in range(C):
                    col = which * D + m * P
                    mm = hi_lo(dst[:, m * TOK:(m + 1) * TOK], lambda i, c: w1[i][:, c, col:col + P],
                               lambda j, c: h1[j][:, c, :])
                return mm

            def v_product(dst, slot):
                h1, w1 = (h1_hi[slot], h1_lo[slot]), (wq_hi, wq_lo)
                for b in range(PAIR):
                    mm = hi_lo(dst[:, b * D:(b + 1) * D], lambda i, c: h1[i][:, c, b * N:(b + 1) * N],
                               lambda j, c: w1[j][:, c, 2 * D:3 * D])
                return mm

            def scores(b, half, slot, dst):
                d = dst[:, :].rearrange("p (h n) -> p h n", n=N)
                pe.matmul(d, ident_bf[:, :], mask_add[:, :].unsqueeze(1).broadcast_to([P, HC, N]),
                          start=True, stop=False, skip_group_check=True)
                for h in range(HC):
                    mm = pe.matmul(d[:, h, :], stack[slot][:, 0, h, half, b * N:(b + 1) * N],
                                   stack[slot][:, 1, h, half, b * N:(b + 1) * N],
                                   start=False, stop=True, skip_group_check=True)
                return mm

            def turn_p(b, half, dst):
                for h in range(HC):
                    mm = pe.transpose(dst[:, h * N:(h + 1) * N], p[:, b, half * HC + h, :], ident[:, :])
                return mm

            pe.wait_ge(pool_const, 2)

            def step(s):
                t = s.t
                if s.on(3):
                    g = t - 3
                    if s.was_on(4):
                        pe.wait_ge(v_ready, t - 4)
                    elif s.was_on(3):
                        pe.wait_ge(q_lo_ready, t - 3)
                    pe.wait_ge(z1_ready, g + 1)
                    transposed(bk[5], z1).then_inc(z1_turned, 1)
                if s.on(5):
                    g, slot = t - 5, s.slot(5)
                    if s.was_on(5):
                        pe.wait_ge(p_t11_ready, t - 5)
                    elif s.was_on(1):
                        pe.wait_ge(s_sum_ready, t - 1)
                    pe.wait_ge(stack_landed[slot], 12 * landed(g, slot))
                    scores(0, 1, slot, bk[6]).then_inc(scores01_done, 1)
                if s.on(2):
                    g, slot = t - 2, s.slot(2)
                    if s.edge:
                        if s.was_on(1):
                            pe.wait_ge(p0_t_ready, t - 1)
                        elif s.was_on(5):
                            pe.wait_ge(p_t10_ready, t - 5)
                        elif s.was_on(2):
                            pe.wait_ge(elu_ready, t - 2)
                    pe.wait_ge(p0_t_ready, g + 1)
                    for b in range(PAIR):
                        mm = pe.matmul(bk[7][:, b * D:(b + 1) * D], p0_t[:, b, :], hw[slot][:, b, 0:D], start=True, stop=True)
                    mm.then_inc(att0_done, 1)
                if s.on(1):
                    g = t - 1
                    if s.was_on(3):
                        pe.wait_ge(k_lo_ready, t - 3)
                    elif s.was_on(6):
                        pe.wait_ge(o_ready, t - 6)
                    elif s.was_on(1):
                        pe.wait_ge(hw0_ready, t - 1)
                    pe.wait_ge(h0_lo_ready, g + 1)
                    if s.first(1):
                        pe.wait_ge(wx_ready, 1)
                    gat_product(bk[1], 0).then_inc(hw0_done, 1)
                if s.on(5):
                    g, slot = t - 5, s.slot(5)
                    if s.was_on(5):
                        pe.wait_ge(inv_t_ready, t - 5)
                    pe.wait_ge(stack_landed[slot], 12 * landed(g, slot))
                    scores(1, 1, slot, bk[0]).then_inc(scores11_done, 1)
                if s.on(5):
                    g, slot = t - 5, s.slot(5)
                    if s.edge:
                        if s.was_on(0):
                            pe.wait_ge(h0_lo_ready, t)
                        elif s.was_on(5):
                            pe.wait_ge(p00_ready, t - 5)
                    pe.wait_ge(stack_landed[slot], 12 * landed(g, slot))
                    if s.first(5):
                        pe.wait_ge(mask_ready, 1)
                    scores(0, 0, slot, bk[3]).then_inc(scores00_done, 1)
                if s.on(6):
                    g, slot = t - 6, s.slot(6)
                    if s.on(1):
                        pe.wait_ge(hw0_ready, t)
                    elif s.was_on(3):
                        pe.wait_ge(k_lo_ready, t - 3)
                    elif s.was_on(6):
                        pe.wait_ge(o_ready, t - 6)
                    pe.wait_ge(v_ready, g + 1)
                    pe.wait_ge(p_t00_ready, g + 1)
                    pe.wait_ge(p_t01_ready, g + 1)
                    pe.wait_ge(p_t10_ready, g + 1)
                    pe.wait_ge(p_t11_ready, g + 1)
                    for b in range(PAIR):
                        for c in range(C):
                            for h in range(HC):
                                hh = c * HC + h
                                mm = pe.matmul(bk[1][h * HD:(h + 1) * HD, (b * C + c) * N:(b * C + c + 1) * N],
                                               v[slot][:, b, hh * HD:(hh + 1) * HD], p_t[:, b, hh, :], start=True, stop=True)
                    mm.then_inc(av_done, 1)
                if s.on(1):
                    g = t - 1
                    if s.edge:
                        if s.was_on(6):
                            pe.wait_ge(y_ready, t - 6)
                        elif s.was_on(1):
                            pe.wait_ge(hw1_ready, t - 1)
                    pe.wait_ge(h0_lo_ready, g + 1)
                    if s.first(1):
                        pe.wait_ge(wx_ready, 1)
                    gat_product(bk[2], 1).then_inc(hw1_done, 1)
                if s.on(3):
                    g, slot = t - 3, s.slot(3)
                    if s.edge:
                        if s.on(3):
                            pe.wait_ge(h1_lo_ready, t - 2)
                        elif s.was_on(4):
                            pe.wait_ge(v_ready, t - 4)
                        elif s.was_on(3):
                            pe.wait_ge(q_lo_ready, t - 3)
                    pe.wait_ge(h1_lo_ready, g + 1)
                    if s.first(3):
                        pe.wait_ge(w_ready, 1)
                    qk_product(bk[5], slot, 0).then_inc(q_done, 1)
                if s.on(5):
                    g = t - 5
                    if s.edge:
                        if s.on(2):
                            pe.wait_ge(elu_ready, t - 1)
                        elif s.was_on(1):
                            pe.wait_ge(p0_t_ready, t - 1)
                        elif s.was_on(5):
                            pe.wait_ge(p_t10_ready, t - 5)
                    pe.wait_ge(p10_ready, g + 1)
                    turn_p(1, 0, bk[7]).then_inc(p10_turned, 1)
                if s.on(5):
                    g = t - 5
                    if s.edge:
                        if s.was_on(4):
                            pe.wait_ge(p10_ready, t - 4)
                        elif s.was_on(5):
                            pe.wait_ge(p_t00_ready, t - 5)
                    pe.wait_ge(p01_ready, g + 1)
                    turn_p(0, 1, bk[4]).then_inc(p01_turned, 1)
                if s.on(1):
                    g, slot = t - 1, s.slot(1)
                    if s.edge:
                        if s.on(5):
                            pe.wait_ge(p01_ready, t - 4)
                        elif s.was_on(5):
                            pe.wait_ge(p_t11_ready, t - 5)
                        elif s.was_on(1):
                            pe.wait_ge(s_sum_ready, t - 1)
                    pe.wait_ge(hw0_ready, g + 1)
                    pe.wait_ge(hw1_ready, g + 1)
                    for b in range(PAIR):
                        mm = pe.transpose(bk[6][:, b * N:(b + 1) * N], hw[slot][:, b, D + 1:D + 2].broadcast_to([P, N]), ident[:, :])
                    mm.then_inc(s2_turned, 1)
                if s.on(3):
                    g, slot = t - 3, s.slot(3)
                    if s.on(6):
                        pe.wait_ge(o_ready, t - 5)
                    elif s.on(1):
                        pe.wait_ge(hw0_ready, t)
                    elif s.was_on(3):
                        pe.wait_ge(k_lo_ready, t - 3)
                    pe.wait_ge(h1_lo_ready, g + 1)
                    if s.first(3):
                        pe.wait_ge(w_ready, 1)
                    qk_product(bk[1], slot, 1).then_inc(k_done, 1)
                if s.on(6):
                    g = t - 6
                    if s.edge:
                        if s.on(1):
                            pe.wait_ge(hw1_ready, t)
                        elif s.was_on(6):
                            pe.wait_ge(y_ready, t - 6)
                    pe.wait_ge(o_ready, g + 1)
                    if s.first(6):
                        pe.wait_ge(bias_ready, 1)
                    for b in range(PAIR):
                        d = bk[2][:, b * D:(b + 1) * D]
                        pe.matmul(d, bias_pick[:, :], bias_parts[:, :], start=True, stop=False)
                        for c in range(C):
                            mm = pe.matmul(d, o_t[:, (b * C + c) * N:(b * C + c + 1) * N], wp[:, c, :], start=False,
                                           stop=(c == C - 1))
                    mm.then_inc(proj_done, 1)
                if s.on(5):
                    g = t - 5
                    if s.on(5):
                        pe.wait_ge(p_t01_ready, t - 4)
                    elif s.was_on(4):
                        pe.wait_ge(p10_ready, t - 4)
                    elif s.was_on(5):
                        pe.wait_ge(p_t00_ready, t - 5)
                    pe.wait_ge(p00_ready, g + 1)
                    turn_p(0, 0, bk[4]).then_inc(p00_turned, 1)
                if s.on(0):
                    g = t
                    if s.edge:
                        if s.on(5):
                            pe.wait_ge(p00_ready, t - 4)
                        elif s.was_on(0):
                            pe.wait_ge(h0_lo_ready, t)
                    pe.wait_ge(z0_ready, g + 1)
                    transposed(bk[3], z0).then_inc(z0_turned, 1)
                if s.on(4):
                    g, slot = t - 4, s.slot(4)
                    if s.edge:
                        if s.on(3):
                            pe.wait_ge(q_lo_ready, t - 2)
                        elif s.was_on(4):
                            pe.wait_ge(v_ready, t - 4)
                    pe.wait_ge(h1_lo_ready, g + 1)
                    if s.first(4):
                        pe.wait_ge(w_ready, 1)
                    v_product(bk[5], slot).then_inc(v_done, 1)
                if s.on(5):
                    g = t - 5
                    if s.edge:
                        if s.on(1):
                            pe.wait_ge(s_sum_ready, t)
                        elif s.on(5):
                            pe.wait_ge(p01_ready, t - 4)
                        elif s.was_on(5):
                            pe.wait_ge(p_t11_ready, t - 5)
                    pe.wait_ge(p11_ready, g + 1)
                    turn_p(1, 1, bk[6]).then_inc(p11_turned, 1)
                if s.on(5):
                    g = t - 5
                    if s.edge:
                        if s.on(5):
                            pe.wait_ge(p11_ready, t - 4)
                        elif s.was_on(5):
                            pe.wait_ge(inv_t_ready, t - 5)
                    pe.wait_ge(inv_ready, g + 1)
                    for k in range(PAIR * C):
                        mm = pe.transpose(bk[0][:, k * N:(k + 1) * N],
                                          inv_rep[:, k * HC:(k + 1) * HC, :].rearrange("p h d -> p (h d)"), ident[:, :])
                    mm.then_inc(inv_turned, 1)
                if s.on(1):
                    g = t - 1
                    if s.edge:
                        if s.on(5):
                            pe.wait_ge(p_t10_ready, t - 4)
                        elif s.on(2):
                            pe.wait_ge(elu_ready, t - 1)
                        elif s.was_on(1):
                            pe.wait_ge(p0_t_ready, t - 1)
                    pe.wait_ge(p0_ready, g + 1)
                    for b in range(PAIR):
                        mm = pe.transpose(bk[7][:, b * N:(b + 1) * N], p0[:, b, :], ident[:, :])
                    mm.then_inc(p0_turned, 1)
                if s.on(4):
                    g, slot = t - 4, s.slot(4)
                    if s.on(5):
                        pe.wait_ge(p_t00_ready, t - 4)
                    elif s.was_on(4):
                        pe.wait_ge(p10_ready, t - 4)
                    pe.wait_ge(stack_landed[slot], 12 * landed(g, slot))
                    scores(1, 0, slot, bk[4]).then_inc(scores10_done, 1)

            pipeline(pe, step)

        @block.scalar
        def _(act):
            def exp_scores(b, half, src):
                for h in range(HC):
                    hh = half * HC + h
                    ins = act.activation(p[:, b, hh, :], src[:, h * N:(h + 1) * N], ACT.Exp,
                                         bias=neg_max[:, b, hh:hh + 1], accum_out=sums[:, b, hh:hh + 1])
                return ins

            def step(s):
                t = s.t
                if s.first(0):
                    act.wait_ge(late_loaded, LATE)
                    act.activation(flat(wq_hi), flat(wq), ACT.Copy).then_inc(w_hi_ready, 1)
                if s.on(6):
                    g = t - 6
                    act.wait_ge(p11_turned, g + 1)
                    act.activation(turned_p(1, 1), bk[6][:, :], ACT.Copy).then_inc(p_t11_ready, 1)
                if s.on(6):
                    g = t - 6
                    act.wait_ge(inv_turned, g + 1)
                    act.activation(inv_t[:, :], bk[0][:, :], ACT.Copy).then_inc(inv_t_ready, 1)
                if s.on(7):
                    g = t - 7
                    act.wait_ge(shift_ready[2], g + 1)
                    act.wait_ge(res_ready, g + 1)
                    for b in range(PAIR):
                        ins = act.activation(y[:, b, :], bk[2][:, b * D:(b + 1) * D], ACT.Identity, scale=rstd[2][:, b:b + 1],
                                             bias=shift[2][:, b:b + 1])
                    ins.then_inc(y_ready, 1)
                if s.on(2):
                    g = t - 2
                    act.wait_ge(att0_done, g + 1)
                    for b in range(PAIR):
                        ins = act.activation(exp_h[:, b, :], bk[7][:, b * D:(b + 1) * D], ACT.Exp, scale=inv_sum0[:, b:b + 1])
                    ins.then_inc(exp_ready, 1)
                if s.on(1):
                    g, slot = t - 1, s.slot(1)
                    act.wait_ge(hw0_done, g + 1)
                    act.activation(hw[slot][:, 0, :], bk[1][:, 0:DS], ACT.Copy).then_inc(hw0_ready, 1)
                if s.on(3):
                    g, slot = t - 3, s.slot(3)
                    act.wait_ge(z1_turned, g + 1)
                    act.activation(flat(h1_hi[slot]), bk[5][:, :], ACT.Relu).then_inc(h1_hi_ready, 1)
                if s.on(5):
                    g = t - 5
                    act.wait_ge(max10_ready, g + 1)
                    exp_scores(1, 0, bk[4]).then_inc(p10_ready, 1)
                if s.on(5):
                    g = t - 5
                    act.wait_ge(max01_ready, g + 1)
                    exp_scores(0, 1, bk[6]).then_inc(p01_ready, 1)
                if s.on(1):
                    g, slot = t - 1, s.slot(1)
                    act.wait_ge(hw1_done, g + 1)
                    act.activation(hw[slot][:, 1, :], bk[2][:, 0:DS], ACT.Copy).then_inc(hw1_ready, 1)
                if s.on(3):
                    g, slot = t - 3, s.slot(3)
                    act.wait_ge(q_done, g + 1)
                    act.activation(flat4(qk[slot][:, 0, :, :]), bk[5][:, :], ACT.Copy, scale=SCALE).then_inc(q_hi_ready, 1)
                if s.on(5):
                    g = t - 5
                    act.wait_ge(p10_turned, g + 1)
                    act.activation(turned_p(1, 0), bk[7][:, :], ACT.Copy).then_inc(p_t10_ready, 1)
                if s.on(1):
                    g, slot = t - 1, s.slot(1)
                    act.wait_ge(s2_turned, g + 1)
                    for b in range(PAIR):
                        ins = act.activation(s_sum[:, b, :], bk[6][:, b * N:(b + 1) * N], ACT.Identity, bias=hw[slot][:, b, D:D + 1])
                    ins.then_inc(s_sum_ready, 1)
                if s.on(5):
                    g = t - 5
                    act.wait_ge(max00_ready, g + 1)
                    exp_scores(0, 0, bk[3]).then_inc(p00_ready, 1)
                if s.on(5):
                    g = t - 5
                    act.wait_ge(max11_ready, g + 1)
                    exp_scores(1, 1, bk[0]).then_inc(p11_ready, 1)
                if s.on(0):
                    g = t
                    act.wait_ge(z0_turned, g + 1)
                    act.activation(flat(h0_hi), bk[3][:, :], ACT.Relu).then_inc(h0_hi_ready, 1)
                if s.on(1):
                    g = t - 1
                    act.wait_ge(max0_ready, g + 1)
                    for b in range(PAIR):
                        ins = act.activation(p0[:, b, :], masked[:, b, :], ACT.Exp, bias=neg_max0[:, b:b + 1],
                                             accum_out=sum0[:, b:b + 1])
                    ins.then_inc(p0_ready, 1)
                if s.on(3):
                    g, slot = t - 3, s.slot(3)
                    act.wait_ge(k_done, g + 1)
                    act.activation(flat4(qk[slot][:, 2, :, :]), bk[1][:, :], ACT.Copy).then_inc(k_hi_ready, 1)
                if s.on(4):
                    g, slot = t - 4, s.slot(4)
                    act.wait_ge(v_done, g + 1)
                    act.activation(v[slot][:, :, :].rearrange("p b d -> p (b d)"), bk[5][:, :], ACT.Copy).then_inc(v_ready, 1)

            pipeline(act, step)

        @block.vector
        def _(dve):
            def prepare_gat():
                dve.wait_ge(early_loaded, EARLY)
                n = 0
                for k in range(2):
                    for c in range(C):
                        if n:
                            dve.wait_ge(w_steps, n)
                        dve.tensor_tensor_reduce(a_scratch[:, :], wx[:, c, 0:D], a_rows[:, k, :], 1.0, 0.0, ALU.mult,
                                                 ALU.add, wx[:, c, D + k:D + k + 1]).then_inc(w_steps, 1)
                        n += 1
                dve.wait_ge(w_steps, n)
                dve.tensor_copy(wx_hi[:, :, :], wx[:, :, :]).then_inc(w_steps, 1)
                dve.wait_ge(w_steps, n + 1)
                dve.tensor_tensor(wx_lo[:, :, :], wx[:, :, :], wx_hi[:, :, :].bitcast(F32),
                                  ALU.subtract).then_inc(wx_ready, 1)
                dve.tensor_scalar(mask_add[:, :], adj_sb[:, :], 0.0, MASKED, ALU.is_equal, ALU.mult).then_inc(mask_ready, 1)

            def split_bias():
                dve.wait_ge(late_loaded, LATE)
                dve.memset(bias_pick[:, :], 1.0 / 32)
                dve.tensor_copy(bias_parts[0:32, :], bias_rows[0:32, :])
                dve.tensor_copy(bias_cast[:, 0, :], bias_rows[:, :]).then_inc(bias_steps, 1)
                dve.wait_ge(bias_steps, 1)
                dve.tensor_tensor(bias_rest[:, 0, :], bias_rows[:, :], bias_cast[:, 0, :],
                                  ALU.subtract).then_inc(bias_steps, 1)
                dve.wait_ge(bias_steps, 2)
                dve.tensor_copy(bias_parts[32:64, :], bias_rest[32:64, 0, :])
                dve.tensor_copy(bias_cast[:, 1, :], bias_rest[:, 0, :]).then_inc(bias_steps, 1)
                dve.wait_ge(bias_steps, 3)
                dve.tensor_tensor(bias_rest[:, 1, :], bias_rest[:, 0, :], bias_cast[:, 1, :],
                                  ALU.subtract).then_inc(bias_steps, 1)
                dve.wait_ge(bias_steps, 4)
                dve.tensor_copy(bias_parts[64:96, :], bias_rest[64:96, 1, :]).then_inc(bias_ready, 1)

            def layer_stats(k, g, src):
                for b in range(PAIR):
                    ins = dve.bn_stats(stats[k][:, b, :], src(b))
                ins.then_inc(stats_ready[k], 1)
                dve.wait_ge(stats_ready[k], g + 1)
                dve.memset(beat[:, :], 0.0)
                for b in range(PAIR):
                    ins = dve.bn_aggr(moments[k][:, b, :], stats[k][:, b, :])
                ins.then_inc(moments_ready[k], 1)

            def maxima(b, half, src):
                return dve.tensor_reduce(neg_max[:, b, half * HC:(half + 1) * HC],
                                         src[:, :].rearrange("p (h n) -> p h n", n=N), AX_X, ALU.max, negate=True)

            def rest(lo, src, hi, op, scalar):
                return dve.scalar_tensor_tensor(out=flat4(lo), in0=src, scalar=scalar, in1=flat4(hi),
                                                op0=op, op1=ALU.subtract)

            dve.wait_ge(pool_const, 2)

            def step(s):
                t = s.t
                if s.on(1):
                    g = t - 1
                    dve.wait_ge(h0_hi_ready, g + 1)
                    rest(h0_lo[:, :, :], bk[3][:, :], h0_hi[:, :, :].bitcast(F32), ALU.max, 0.0).then_inc(h0_lo_ready, 1)
                if s.on(4):
                    g, slot = t - 4, s.slot(4)
                    dve.wait_ge(k_hi_ready, g + 1)
                    dve.tensor_tensor(flat4(qk[slot][:, 3, :, :]), bk[1][:, :], flat4(qk[slot][:, 2, :, :]),
                                      ALU.subtract).then_inc(k_lo_ready, 1)
                if s.on(5):
                    g = t - 5
                    dve.wait_ge(scores10_done, g + 1)
                    maxima(1, 0, bk[4]).then_inc(max10_ready, 1)
                if s.on(5):
                    g = t - 5
                    dve.wait_ge(scores01_done, g + 1)
                    maxima(0, 1, bk[6]).then_inc(max01_ready, 1)
                if s.on(2):
                    g = t - 2
                    dve.wait_ge(exp_ready, g + 1)
                    dve.tensor_scalar(exp_m1[:, :, :], exp_h[:, :, :], 1.0, 1.0, ALU.min, ALU.subtract).then_inc(exp_m1_ready, 1)
                if s.on(2):
                    g = t - 2
                    dve.wait_ge(exp_m1_ready, g + 1)
                    for b in range(PAIR):
                        ins = dve.scalar_tensor_tensor(out=elu[:, b * D:(b + 1) * D], in0=bk[7][:, b * D:(b + 1) * D],
                                                       scalar=inv_sum0[:, b:b + 1], in1=exp_m1[:, b, :], op0=ALU.mult, op1=ALU.max)
                    ins.then_inc(elu_ready, 1)
                if s.on(3):
                    g, slot = t - 3, s.slot(3)
                    dve.wait_ge(h1_hi_ready, g + 1)
                    rest(h1_lo[slot][:, :, :], bk[5][:, :], h1_hi[slot][:, :, :].bitcast(F32), ALU.max, 0.0).then_inc(h1_lo_ready, 1)
                if s.on(0):
                    g, slot = t, s.slot(0)
                    dve.wait_ge(x_loaded[slot], landed(g, slot))
                    layer_stats(0, g, lambda b: xs_of(g, b))
                    if s.first(0):
                        prepare_gat()
                if s.on(5):
                    g = t - 5
                    dve.wait_ge(scores00_done, g + 1)
                    maxima(0, 0, bk[3]).then_inc(max00_ready, 1)
                if s.on(6):
                    g = t - 6
                    dve.wait_ge(av_done, g + 1)
                    dve.wait_ge(inv_t_ready, g + 1)
                    dve.tensor_tensor(o_t[:, :], bk[1][:, :], inv_t[:, :], ALU.mult).then_inc(o_ready, 1)
                if s.on(7):
                    g, slot = t - 7, s.slot(7)
                    dve.wait_ge(out_stored[slot], landed(g, slot))
                    dve.wait_ge(y_gamma_ready, g + 1)
                    dve.tensor_tensor(out_sb[slot][:, :], y_gamma[:, :, :].rearrange("p b d -> p (b d)"), res[:, :],
                                      ALU.add).then_inc(out_ready, 1)
                if s.on(3):
                    g, slot = t - 3, s.slot(3)
                    dve.wait_ge(q_hi_ready, g + 1)
                    rest(qk[slot][:, 1, :, :], bk[5][:, :], qk[slot][:, 0, :, :], ALU.mult, SCALE).then_inc(q_lo_ready, 1)
                if s.on(5):
                    g = t - 5
                    dve.wait_ge(scores11_done, g + 1)
                    maxima(1, 1, bk[0]).then_inc(max11_ready, 1)
                if s.on(5):
                    g = t - 5
                    dve.wait_ge(p01_turned, g + 1)
                    dve.tensor_copy(turned_p(0, 1), bk[4][:, :]).then_inc(p_t01_ready, 1)
                if s.on(1):
                    g = t - 1
                    dve.wait_ge(s_sum_ready, g + 1)
                    dve.scalar_tensor_tensor(out=leaky[:, :, :], in0=s_sum[:, :, :], scalar=LEAKY_SLOPE, in1=s_sum[:, :, :],
                                             op0=ALU.mult, op1=ALU.max).then_inc(leaky_ready, 1)
                if s.on(2):
                    g = t - 2
                    dve.wait_ge(x1_ready, g + 1)
                    layer_stats(1, g, lambda b: x1[:, b * D:(b + 1) * D])
                if s.on(1):
                    g = t - 1
                    dve.wait_ge(masked_ready, g + 1)
                    dve.tensor_reduce(neg_max0[:, :], masked[:, :, :], AX_X, ALU.max, negate=True).then_inc(max0_ready, 1)
                if s.on(6):
                    g = t - 6
                    dve.wait_ge(proj_done, g + 1)
                    layer_stats(2, g, lambda b: bk[2][:, b * D:(b + 1) * D])
                if s.on(5):
                    g = t - 5
                    dve.wait_ge(p00_ready, g + 1)
                    dve.wait_ge(p01_ready, g + 1)
                    dve.wait_ge(p10_ready, g + 1)
                    dve.wait_ge(p11_ready, g + 1)
                    dve.reciprocal(inv_sum[:, :], sums[:, :, :].rearrange("p b h -> p (b h)")).then_inc(recip_done, 1)
                    dve.wait_ge(recip_done, g + 1)
                    dve.tensor_copy(inv_rep[:, :, :], inv_sum[:, :].unsqueeze(2).broadcast_to([P, PAIR * H, HD])).then_inc(inv_ready, 1)
                if s.on(5):
                    g = t - 5
                    dve.wait_ge(p00_turned, g + 1)
                    dve.tensor_copy(turned_p(0, 0), bk[4][:, :]).then_inc(p_t00_ready, 1)
                if s.on(6):
                    g = t - 6
                    dve.wait_ge(proj_done, g + 1)
                    dve.wait_ge(x1b_ready, g + 1)
                    dve.tensor_tensor(res[:, :], bk[2][:, :], xs_of(g), ALU.add).then_inc(res_ready, 1)
                if s.on(1):
                    g = t - 1
                    dve.wait_ge(p0_ready, g + 1)
                    dve.tensor_scalar(beta_sum0[:, :], sum0[:, :], gbeta[:, 0:1], None, ALU.mult)
                    dve.reciprocal(inv_sum0[:, :], sum0[:, :]).then_inc(inv0_ready, 1)
                if s.on(1):
                    g = t - 1
                    dve.wait_ge(p0_turned, g + 1)
                    dve.wait_ge(inv0_ready, g + 1)
                    for b in range(PAIR):
                        ins = dve.scalar_tensor_tensor(out=p0_t[:, b, :], in0=ident[:, :], scalar=beta_sum0[:, b:b + 1],
                                                       in1=bk[7][:, b * N:(b + 1) * N], op0=ALU.mult, op1=ALU.add)
                    ins.then_inc(p0_t_ready, 1)
                if s.first(1):
                    split_bias()

            pipeline(dve, step)

        @block.gpsimd
        def _(pool):
            pool.memset(minus_half[:, :], -0.5)
            pool.memset(minus_one[:, :], -1.0)
            pool.memset(eps[:, :], LN_EPS)
            pool.memset(ident[:, :], 0.0).then_inc(ident_cleared, 1)
            pool.wait_ge(ident_cleared, 1)
            pool.affine_select(out=ident[:, :], in_=ident[:, :], compare_op=ALU.not_equal, fill=1.0, base=0,
                               pattern=[[-1, P]], channel_multiplier=1).then_inc(pool_const, 1)
            pool.wait_ge(pool_const, 1)
            pool.tensor_copy(ident_bf[:, :], ident[:, :]).then_inc(pool_const, 1)
            pool.wait_ge(pool_const, 2)

            def norm(k, g):
                pool.wait_ge(moments_ready[k], g + 1)
                pool.tensor_tensor(var_eps[k][:, :], moments[k][:, :, 1], eps[:, :],
                                   ALU.add).then_inc(eps_added[k], 1)
                pool.tensor_tensor(neg_mean[k][:, :], moments[k][:, :, 0], minus_one[:, :],
                                   ALU.mult).then_inc(neg_mean_ready[k], 1)
                pool.wait_ge(eps_added[k], g + 1)
                pool.tensor_tensor(rstd[k][:, :], var_eps[k][:, :], minus_half[:, :],
                                   ALU.pow).then_inc(rstd_ready[k], 1)
                pool.wait_ge(rstd_ready[k], g + 1)
                pool.wait_ge(neg_mean_ready[k], g + 1)
                pool.tensor_tensor(shift[k][:, :], neg_mean[k][:, :], rstd[k][:, :],
                                   ALU.mult).then_inc(shift_ready[k], 1)

            pool.wait_ge(early_loaded, EARLY)

            def step(s):
                t = s.t
                if s.on(7):
                    g = t - 7
                    pool.wait_ge(moments_ready[2], g + 1)
                    norm(2, g)
                if s.on(3):
                    g = t - 3
                    if s.first(3):
                        pool.wait_ge(late_loaded, LATE)
                    pool.tensor_tensor(pairs(xs_of(g)), pairs(x1[:, :]), lnb[:, :].unsqueeze(1).broadcast_to([P, PAIR, D]),
                                       ALU.add).then_inc(x1b_ready, 1)
                if s.on(7):
                    g = t - 7
                    pool.wait_ge(y_ready, g + 1)
                    pool.tensor_tensor(y_gamma[:, :, :], y[:, :, :], gamma[:, :].unsqueeze(1).broadcast_to([P, PAIR, D]),
                                       ALU.mult).then_inc(y_gamma_ready, 1)
                if s.on(2):
                    g = t - 2
                    if s.from_group(1, 2):
                        pool.wait_ge(x1b_ready, g)
                    pool.wait_ge(elu_ready, g + 1)
                    pool.tensor_tensor(pool_beat[:, :], eps[:, :], eps[:, :], ALU.add)
                    pool.tensor_tensor(x1[:, :], elu[:, :], xs_of(g), ALU.add).then_inc(x1_ready, 1)
                if s.on(0):
                    g = t
                    pool.wait_ge(moments_ready[0], g + 1)
                    norm(0, g)
                    pool.tensor_tensor(pairs(centred[:, :]), pairs(xs_of(g)), neg_mean[0][:, :].unsqueeze(2).broadcast_to([P, PAIR, D]),
                                       ALU.add).then_inc(centred_ready, 1)
                    pool.wait_ge(centred_ready, g + 1)
                    pool.tensor_tensor(pairs(z0[:, :]), pairs(centred[:, :]), rstd[0][:, :].unsqueeze(2).broadcast_to([P, PAIR, D]),
                                       ALU.mult).then_inc(z0_ready, 1)
                if s.on(1):
                    g = t - 1
                    pool.wait_ge(leaky_ready, g + 1)
                    pool.tensor_tensor(masked[:, :, :], leaky[:, :, :], adj_sb[:, :].unsqueeze(1).broadcast_to([P, PAIR, N]),
                                       ALU.mult).then_inc(masked_ready, 1)
                if s.on(2):
                    g = t - 2
                    pool.wait_ge(moments_ready[1], g + 1)
                    norm(1, g)
                    for b in range(PAIR):
                        ins = pool.tensor_scalar(z1[:, b * D:(b + 1) * D], x1[:, b * D:(b + 1) * D], neg_mean[1][:, b:b + 1],
                                                 rstd[1][:, b:b + 1], ALU.add, ALU.mult)
                    ins.then_inc(z1_ready, 1)
                if s.first(0):
                    pool.wait_ge(w_hi_ready, 1)
                    pool.tensor_tensor(flat(wq_lo), flat(wq), flat4(wq_hi[:, :, :].bitcast(F32)),
                                       ALU.subtract).then_inc(w_ready, 1)

            pipeline(pool, step)


_INS = ['x', 'adj', 'L0_gnn_W', 'L0_gnn_a', 'L0_gnn_beta', 'L1_gnn_w_qkv', 'L1_gnn_w_proj', 'L1_gnn_b_proj',
        'L1_gnn_ln_gamma', 'L1_gnn_ln_beta']


def kernel(**inputs):
    import numpy as _np
    import concourse.bacc as _bacc
    from concourse import mybir as _mybir
    from concourse.bass_utils import run_bass_kernel_spmd as _run

    nc = _bacc.Bacc("TRN2", target_bir_lowering=False, num_devices=1)
    arrays, args = {}, []
    for name in _INS:
        a = _np.ascontiguousarray(inputs[name])
        arrays[f"in_{name}_dram"] = a
        args.append(nc.dram_tensor(f"in_{name}_dram", a.shape, _mybir.dt.from_np(a.dtype), kind="ExternalInput").ap())
    shape = inputs['x'].shape
    args.append(nc.dram_tensor("out_0_dram", shape, _mybir.dt.float32, kind="ExternalOutput").ap())
    gat_transformer(nc, *args)
    r = _run(nc, [arrays], core_ids=[0])
    return r.results[0]["out_0_dram"]
```

```python
from contextlib import ExitStack

import concourse.bass as bass
from concourse import mybir

ALU = mybir.AluOpType
ACT = mybir.ActivationFunctionType
AX_X = mybir.AxisListType.X
F32 = mybir.dt.float32
F32R = mybir.dt.float32r
F16 = mybir.dt.float16
BF16 = mybir.dt.bfloat16

P = 128
LN_EPS = 1e-5
LEAKY_SLOPE = 0.2
MASKED = -1e30

LAST_LAG = 7


def gat_transformer(nc, x, adj, gat_w, gat_a, gat_beta, w_qkv, w_proj, b_proj, ln_gamma, ln_beta, out):
    B, N, D = x.shape
    C = D // P
    H = 8
    HD = D // H
    HC = P // HD
    SCALE = float(HD) ** -0.5
    PAIR = 2
    NG = B // PAIR
    TOK = PAIR * N
    GW = PAIR * D
    DS = D + 2
    STACK = 3 * HD
    assert N == P and C == 2 and NG > LAST_LAG

    with ExitStack() as ctx:
        def sb(name, shape, dt=F32):
            return ctx.enter_context(nc.sbuf_tensor(name, shape, dt))

        def bank(name):
            return ctx.enter_context(nc.psum_tensor(name, [P, 512], F32))

        def sem(name):
            return ctx.enter_context(nc.semaphore(name))

        def two(make, name, *args):
            return [make(f"{name}{i}", *args) for i in range(2)]

        ident = sb("ident", [P, P])
        ident_bf = sb("ident_bf", [P, P], BF16)
        adj_sb = sb("adj_sb", [P, N])
        mask_add = sb("mask_add", [P, N], BF16)
        wx = sb("wx", [P, C, DS])
        wx_hi = sb("wx_hi", [P, C, DS], F32R)
        wx_lo = sb("wx_lo", [P, C, DS], F32R)
        wq = sb("wq", [P, C, 3 * D])
        wq_hi = sb("wq_hi", [P, C, 3 * D], F32R)
        wq_lo = sb("wq_lo", [P, C, 3 * D], F32R)
        wp = sb("wp", [P, C, D])
        a_rows = sb("a_rows", [P, 2, D])
        a_scratch = sb("a_scratch", [P, D])
        gbeta = sb("gbeta", [P, 1])
        bias_rows = sb("bias_rows", [P, D])
        bias_cast = sb("bias_cast", [P, 2, D], BF16)
        bias_rest = sb("bias_rest", [P, 2, D])
        bias_parts = sb("bias_parts", [3 * 32, D], BF16)
        bias_pick = sb("bias_pick", [3 * 32, P], BF16)
        gamma = sb("gamma", [P, D])
        lnb = sb("lnb", [P, D])
        minus_half = sb("minus_half", [P, PAIR])
        minus_one = sb("minus_one", [P, PAIR])
        eps = sb("eps", [P, PAIR])
        beat, pool_beat = sb("beat", [P, 1]), sb("pool_beat", [P, PAIR])

        xs = sb("xs", [P, NG * GW])
        stats = [sb(f"stats{k}", [P, PAIR, 6]) for k in range(3)]
        moments = [sb(f"moments{k}", [P, PAIR, 2]) for k in range(3)]
        var_eps = [sb(f"var_eps{k}", [P, PAIR]) for k in range(3)]
        neg_mean = [sb(f"neg_mean{k}", [P, PAIR]) for k in range(3)]
        rstd = [sb(f"rstd{k}", [P, PAIR]) for k in range(3)]
        shift = [sb(f"shift{k}", [P, PAIR]) for k in range(3)]
        centred = sb("centred", [P, GW])
        z0 = sb("z0", [P, GW])
        h0_hi = sb("h0_hi", [P, C, TOK], F32R)
        h0_lo = sb("h0_lo", [P, C, TOK], F32R)
        hw = two(sb, "hw", [P, PAIR, DS])
        s_sum = sb("s_sum", [P, PAIR, N])
        leaky = sb("leaky", [P, PAIR, N])
        masked = sb("masked", [P, PAIR, N])
        neg_max0 = sb("neg_max0", [P, PAIR])
        p0 = sb("p0", [P, PAIR, N])
        sum0 = sb("sum0", [P, PAIR])
        beta_sum0 = sb("beta_sum0", [P, PAIR])
        inv_sum0 = sb("inv_sum0", [P, PAIR])
        p0_t = sb("p0_t", [P, PAIR, N])
        exp_h = sb("exp_h", [P, PAIR, D])
        exp_m1 = sb("exp_m1", [P, PAIR, D])
        elu = sb("elu", [P, GW])
        x1 = sb("x1", [P, GW])
        z1 = sb("z1", [P, GW])
        h1_hi = two(sb, "h1_hi", [P, C, TOK], F32R)
        h1_lo = two(sb, "h1_lo", [P, C, TOK], F32R)
        qk = two(sb, "qk", [P, 4, C, TOK], F16)
        stack = two(sb, "stack", [STACK, 2, HC, C, TOK], F16)
        v = two(sb, "v", [P, PAIR, D])
        neg_max = sb("neg_max", [P, PAIR, H])
        p = sb("p", [P, PAIR, H, N])
        p_t = sb("p_t", [P, PAIR, H, N])
        sums = sb("sums", [P, PAIR, H])
        inv_sum = sb("inv_sum", [P, PAIR * H])
        inv_rep = sb("inv_rep", [P, PAIR * H, HD])
        inv_t = sb("inv_t", [P, PAIR * C * N])
        o_t = sb("o_t", [P, PAIR * C * N])
        y = sb("y", [P, PAIR, D])
        y_gamma = sb("y_gamma", [P, PAIR, D])
        res = sb("res", [P, GW])
        out_sb = two(sb, "out_sb", [P, GW])

        bk = [bank(f"bank{i}") for i in range(8)]

        early_loaded, late_loaded = sem("early_loaded"), sem("late_loaded")
        pool_const = sem("pool_const")
        ident_cleared = sem("ident_cleared")
        w_steps, bias_steps = sem("w_steps"), sem("bias_steps")
        wx_ready, w_hi_ready, w_ready, bias_ready = sem("wx_ready"), sem("w_hi_ready"), sem("w_ready"), sem("bias_ready")
        mask_ready = sem("mask_ready")
        x_loaded = two(sem, "x_loaded")
        stack_landed = two(sem, "stack_landed")
        out_stored = two(sem, "out_stored")
        stats_ready = [sem(f"stats_ready{k}") for k in range(3)]
        moments_ready = [sem(f"moments_ready{k}") for k in range(3)]
        eps_added = [sem(f"eps_added{k}") for k in range(3)]
        neg_mean_ready = [sem(f"neg_mean_ready{k}") for k in range(3)]
        rstd_ready = [sem(f"rstd_ready{k}") for k in range(3)]
        shift_ready = [sem(f"shift_ready{k}") for k in range(3)]
        recip_done, centred_ready = sem("recip_done"), sem("centred_ready")
        z0_ready = sem("z0_ready")
        z0_turned = sem("z0_turned")
        h0_hi_ready = sem("h0_hi_ready")
        h0_lo_ready = sem("h0_lo_ready")
        hw0_done = sem("hw0_done")
        hw1_done = sem("hw1_done")
        hw0_ready = sem("hw0_ready")
        hw1_ready = sem("hw1_ready")
        s2_turned = sem("s2_turned")
        s_sum_ready = sem("s_sum_ready")
        leaky_ready = sem("leaky_ready")
        masked_ready = sem("masked_ready")
        max0_ready = sem("max0_ready")
        p0_ready = sem("p0_ready")
        inv0_ready = sem("inv0_ready")
        p0_turned = sem("p0_turned")
        p0_t_ready = sem("p0_t_ready")
        att0_done = sem("att0_done")
        exp_ready = sem("exp_ready")
        exp_m1_ready = sem("exp_m1_ready")
        elu_ready = sem("elu_ready")
        x1_ready = sem("x1_ready")
        z1_ready = sem("z1_ready")
        x1b_ready = sem("x1b_ready")
        z1_turned = sem("z1_turned")
        h1_hi_ready = sem("h1_hi_ready")
        h1_lo_ready = sem("h1_lo_ready")
        q_done = sem("q_done")
        k_done = sem("k_done")
        v_done = sem("v_done")
        q_hi_ready = sem("q_hi_ready")
        q_lo_ready = sem("q_lo_ready")
        k_hi_ready = sem("k_hi_ready")
        k_lo_ready = sem("k_lo_ready")
        v_ready = sem("v_ready")
        scores00_done = sem("scores00_done")
        max00_ready = sem("max00_ready")
        p00_ready = sem("p00_ready")
        p00_turned = sem("p00_turned")
        p_t00_ready = sem("p_t00_ready")
        scores01_done = sem("scores01_done")
        max01_ready = sem("max01_ready")
        p01_ready = sem("p01_ready")
        p01_turned = sem("p01_turned")
        p_t01_ready = sem("p_t01_ready")
        scores10_done = sem("scores10_done")
        max10_ready = sem("max10_ready")
        p10_ready = sem("p10_ready")
        p10_turned = sem("p10_turned")
        p_t10_ready = sem("p_t10_ready")
        scores11_done = sem("scores11_done")
        max11_ready = sem("max11_ready")
        p11_ready = sem("p11_ready")
        p11_turned = sem("p11_turned")
        p_t11_ready = sem("p_t11_ready")
        inv_ready = sem("inv_ready")
        inv_turned = sem("inv_turned")
        inv_t_ready = sem("inv_t_ready")
        av_done = sem("av_done")
        o_ready = sem("o_ready")
        proj_done = sem("proj_done")
        res_ready = sem("res_ready")
        y_ready = sem("y_ready")
        y_gamma_ready = sem("y_gamma_ready")
        out_ready = sem("out_ready")

        x_dram = x.rearrange("b n d -> n b d")
        out_dram = out.rearrange("b n d -> n b d")

        def xs_of(g, b=None):
            if b is None:
                return xs[:, bass.ds(g * GW, GW)]
            return xs[:, bass.ds(g * GW + b * D, D)]

        def pairs(ap, w=D):
            return ap.rearrange("p (b w) -> p b w", w=w)

        EARLY, LATE = 16 * 5, 16 * 5

        def flat4(ap):
            return ap.rearrange("p c t -> p (c t)")

        def flat(tile):
            return flat4(tile[:, :, :])

        def turned_p(b, half):
            return p_t[:, b, half * HC:(half + 1) * HC, :].rearrange("p h n -> p (h n)")

        def landed(g, slot):
            return 8 * (g - slot) + 16

        class Step:

            def __init__(self, t, low, high, parity):
                self.t, self.low, self.high, self.parity = t, low, high, parity
                self.edge = low == high

            def on(self, lag):
                return self.low - lag >= 0 and self.high - lag < NG

            def was_on(self, lag):
                return self.low - 1 - lag >= 0 and self.high - 1 - lag < NG

            def first(self, lag):
                return self.low == self.high == lag

            def from_group(self, n, lag):
                return self.low - lag >= n

            def slot(self, lag):
                return (self.parity + lag) % 2

        def pipeline(eng, step):
            lead = LAST_LAG + 1 + (NG - LAST_LAG - 1) % 2
            for t in range(lead):
                step(Step(t, t, t, t % 2))
            with eng.Fori(0, (NG - lead) // 2) as k:
                t = lead + 2 * k
                step(Step(t, lead, NG - 2, lead % 2))
                step(Step(t + 1, lead + 1, NG - 1, (lead + 1) % 2))
            for t in range(NG, NG + LAST_LAG):
                step(Step(t, t, t, t % 2))

        block = ctx.enter_context(nc.Block())

        @block.sync
        def _(sp):
            def broadcast(ap, n):
                return ap.rearrange("(a n) -> a n", a=1).broadcast_to([P, n])

            sp.dma_start(pairs(xs_of(0)), x_dram[:, 0:PAIR, :]).then_inc(x_loaded[0], 16)
            sp.dma_start(wx[:, :, 0:D], gat_w.rearrange("(c p) f -> p c f", p=P)).then_inc(early_loaded, 16)
            for k in range(2):
                a_k = gat_a[k * D:(k + 1) * D, :].rearrange("d a -> (d a)")
                sp.dma_start(a_rows[:, k, :], broadcast(a_k, D)).then_inc(early_loaded, 16)
            sp.dma_start(adj_sb[:, :], adj).then_inc(early_loaded, 16)
            sp.dma_start(gbeta[:, :], broadcast(gat_beta, 1)).then_inc(early_loaded, 16)

            def load_late():
                sp.dma_start(wq[:, :, :], w_qkv.rearrange("(c p) f -> p c f", p=P)).then_inc(late_loaded, 16)
                sp.dma_start(wp[:, :, :], w_proj.rearrange("(c p) f -> p c f", p=P)).then_inc(late_loaded, 16)
                for row, dst in ((b_proj, bias_rows), (ln_gamma, gamma), (ln_beta, lnb)):
                    sp.dma_start(dst[:, :], broadcast(row, D)).then_inc(late_loaded, 16)

            for slot in range(2):
                sp.sem_inc(out_stored[slot], 16)

            def step(s):
                t = s.t
                if s.on(0):
                    g, slot = t, s.slot(0)
                    if s.low >= 2:
                        sp.wait_ge(x_loaded[slot], landed(g - 2, slot))
                    if not s.first(0):
                        sp.dma_start(pairs(xs_of(g)), x_dram[:, bass.ds(g * PAIR, PAIR), :]).then_inc(x_loaded[slot], 16)
                if s.on(4):
                    g, slot = t - 4, s.slot(4)
                    sp.wait_ge(q_lo_ready, g + 1)
                    sp.wait_ge(k_lo_ready, g + 1)
                    for part, picks in enumerate((slice(0, 3, 2), slice(0, 4, 3), slice(1, 3, 1))):
                        for h in range(HC):
                            sp.dma_start(stack[slot][part * HD:(part + 1) * HD, :, h, :, :],
                                         qk[slot][h * HD:(h + 1) * HD, picks, :, :]).then_inc(stack_landed[slot], 16)
                if s.on(7):
                    g, slot = t - 7, s.slot(7)
                    sp.wait_ge(out_ready, g + 1)
                    sp.dma_start(out_dram[:, bass.ds(g * PAIR, PAIR), :], pairs(out_sb[slot][:, :])).then_inc(out_stored[slot], 16)
                if s.first(0):
                    load_late()

            pipeline(sp, step)
            for slot in range(2):
                sp.wait_ge(out_stored[slot], 16 * (NG // 2 + 1))

        @block.tensor
        def _(pe):
            def hi_lo(dst, lhs, rhs):
                n = 0
                for c in range(C):
                    for i, j in ((1, 0), (0, 1), (0, 0)):
                        mm = pe.matmul(dst, lhs(i, c), rhs(j, c), start=(n == 0), stop=(n == 3 * C - 1))
                        n += 1
                return mm

            def transposed(dst, src):
                for b in range(PAIR):
                    for c in range(C):
                        mm = pe.transpose(dst[:, c * TOK + b * N:c * TOK + (b + 1) * N],
                                          src[:, b * D + c * P:b * D + (c + 1) * P], ident[:, :])
                return mm

            def gat_product(dst, b):
                h0, w0 = (h0_hi, h0_lo), (wx_hi, wx_lo)
                return hi_lo(dst[:, 0:DS], lambda i, c: h0[i][:, c, b * N:(b + 1) * N], lambda j, c: w0[j][:, c, :])

            def qk_product(dst, slot, which):
                h1, w1 = (h1_hi[slot], h1_lo[slot]), (wq_hi, wq_lo)
                for m in range(C):
                    col = which * D + m * P
                    mm = hi_lo(dst[:, m * TOK:(m + 1) * TOK], lambda i, c: w1[i][:, c, col:col + P],
                               lambda j, c: h1[j][:, c, :])
                return mm

            def v_product(dst, slot):
                h1, w1 = (h1_hi[slot], h1_lo[slot]), (wq_hi, wq_lo)
                for b in range(PAIR):
                    mm = hi_lo(dst[:, b * D:(b + 1) * D], lambda i, c: h1[i][:, c, b * N:(b + 1) * N],
                               lambda j, c: w1[j][:, c, 2 * D:3 * D])
                return mm

            def scores(b, half, slot, dst):
                d = dst[:, :].rearrange("p (h n) -> p h n", n=N)
                pe.matmul(d, ident_bf[:, :], mask_add[:, :].unsqueeze(1).broadcast_to([P, HC, N]),
                          start=True, stop=False, skip_group_check=True)
                for h in range(HC):
                    mm = pe.matmul(d[:, h, :], stack[slot][:, 0, h, half, b * N:(b + 1) * N],
                                   stack[slot][:, 1, h, half, b * N:(b + 1) * N],
                                   start=False, stop=True, skip_group_check=True)
                return mm

            def turn_p(b, half, dst):
                for h in range(HC):
                    mm = pe.transpose(dst[:, h * N:(h + 1) * N], p[:, b, half * HC + h, :], ident[:, :])
                return mm

            pe.wait_ge(pool_const, 2)

            def step(s):
                t = s.t
                if s.on(1):
                    g = t - 1
                    if s.was_on(4):
                        pe.wait_ge(v_ready, t - 4)
                    elif s.was_on(1):
                        pe.wait_ge(h0_lo_ready, t - 1)
                    pe.wait_ge(z0_ready, g + 1)
                    transposed(bk[0], z0).then_inc(z0_turned, 1)
                if s.on(5):
                    g, slot = t - 5, s.slot(5)
                    if s.was_on(2):
                        pe.wait_ge(elu_ready, t - 2)
                    elif s.was_on(5):
                        pe.wait_ge(p10_ready, t - 5)
                    pe.wait_ge(stack_landed[slot], 12 * landed(g, slot))
                    scores(1, 0, slot, bk[5]).then_inc(scores10_done, 1)
                if s.on(6):
                    g, slot = t - 6, s.slot(6)
                    if s.was_on(1):
                        pe.wait_ge(s_sum_ready, t - 1)
                    elif s.was_on(6):
                        pe.wait_ge(o_ready, t - 6)
                    pe.wait_ge(v_ready, g + 1)
                    pe.wait_ge(p_t00_ready, g + 1)
                    pe.wait_ge(p_t01_ready, g + 1)
                    pe.wait_ge(p_t10_ready, g + 1)
                    pe.wait_ge(p_t11_ready, g + 1)
                    for b in range(PAIR):
                        for c in range(C):
                            for h in range(HC):
                                hh = c * HC + h
                                mm = pe.matmul(bk[6][h * HD:(h + 1) * HD, (b * C + c) * N:(b * C + c + 1) * N],
                                               v[slot][:, b, hh * HD:(hh + 1) * HD], p_t[:, b, hh, :], start=True, stop=True)
                    mm.then_inc(av_done, 1)
                if s.on(5):
                    g, slot = t - 5, s.slot(5)
                    if s.was_on(3):
                        pe.wait_ge(q_lo_ready, t - 3)
                    elif s.was_on(5):
                        pe.wait_ge(p11_ready, t - 5)
                    pe.wait_ge(stack_landed[slot], 12 * landed(g, slot))
                    scores(1, 1, slot, bk[3]).then_inc(scores11_done, 1)
                if s.on(5):
                    g, slot = t - 5, s.slot(5)
                    if s.was_on(3):
                        pe.wait_ge(k_lo_ready, t - 3)
                    elif s.was_on(5):
                        pe.wait_ge(p_t00_ready, t - 5)
                    pe.wait_ge(stack_landed[slot], 12 * landed(g, slot))
                    if s.first(5):
                        pe.wait_ge(mask_ready, 1)
                    scores(0, 0, slot, bk[2]).then_inc(scores00_done, 1)
                if s.on(4):
                    g, slot = t - 4, s.slot(4)
                    if s.on(1):
                        pe.wait_ge(h0_lo_ready, t)
                    elif s.was_on(4):
                        pe.wait_ge(v_ready, t - 4)
                    pe.wait_ge(h1_lo_ready, g + 1)
                    if s.first(4):
                        pe.wait_ge(w_ready, 1)
                    v_product(bk[0], slot).then_inc(v_done, 1)
                if s.on(1):
                    g = t - 1
                    if s.on(6):
                        pe.wait_ge(o_ready, t - 5)
                    elif s.was_on(1):
                        pe.wait_ge(s_sum_ready, t - 1)
                    pe.wait_ge(h0_lo_ready, g + 1)
                    if s.first(1):
                        pe.wait_ge(wx_ready, 1)
                    gat_product(bk[6], 0).then_inc(hw0_done, 1)
                if s.on(6):
                    g = t - 6
                    if s.edge:
                        if s.was_on(6):
                            pe.wait_ge(y_ready, t - 6)
                    pe.wait_ge(o_ready, g + 1)
                    if s.first(6):
                        pe.wait_ge(bias_ready, 1)
                    for b in range(PAIR):
                        d = bk[1][:, b * D:(b + 1) * D]
                        pe.matmul(d, bias_pick[:, :], bias_parts[:, :], start=True, stop=False)
                        for c in range(C):
                            mm = pe.matmul(d, o_t[:, (b * C + c) * N:(b * C + c + 1) * N], wp[:, c, :], start=False,
                                           stop=(c == C - 1))
                    mm.then_inc(proj_done, 1)
                if s.on(5):
                    g = t - 5
                    if s.edge:
                        if s.was_on(5):
                            pe.wait_ge(inv_t_ready, t - 5)
                    pe.wait_ge(p01_ready, g + 1)
                    turn_p(0, 1, bk[7]).then_inc(p01_turned, 1)
                if s.on(5):
                    g = t - 5
                    if s.edge:
                        if s.was_on(4):
                            pe.wait_ge(p01_ready, t - 4)
                        elif s.was_on(5):
                            pe.wait_ge(p_t10_ready, t - 5)
                    pe.wait_ge(p10_ready, g + 1)
                    turn_p(1, 0, bk[4]).then_inc(p10_turned, 1)
                if s.on(2):
                    g = t - 2
                    if s.edge:
                        if s.on(5):
                            pe.wait_ge(p10_ready, t - 4)
                        elif s.was_on(2):
                            pe.wait_ge(elu_ready, t - 2)
                    pe.wait_ge(p0_ready, g + 1)
                    for b in range(PAIR):
                        mm = pe.transpose(bk[5][:, b * N:(b + 1) * N], p0[:, b, :], ident[:, :])
                    mm.then_inc(p0_turned, 1)
                if s.on(1):
                    g = t - 1
                    if s.on(1):
                        pe.wait_ge(hw0_ready, t)
                    elif s.on(6):
                        pe.wait_ge(o_ready, t - 5)
                    elif s.was_on(1):
                        pe.wait_ge(s_sum_ready, t - 1)
                    pe.wait_ge(h0_lo_ready, g + 1)
                    if s.first(1):
                        pe.wait_ge(wx_ready, 1)
                    gat_product(bk[6], 1).then_inc(hw1_done, 1)
                if s.on(3):
                    g = t - 3
                    if s.on(5):
                        pe.wait_ge(p11_ready, t - 4)
                    elif s.was_on(3):
                        pe.wait_ge(q_lo_ready, t - 3)
                    pe.wait_ge(z1_ready, g + 1)
                    transposed(bk[3], z1).then_inc(z1_turned, 1)
                if s.on(5):
                    g = t - 5
                    if s.on(5):
                        pe.wait_ge(p_t01_ready, t - 4)
                    elif s.was_on(5):
                        pe.wait_ge(inv_t_ready, t - 5)
                    pe.wait_ge(p11_ready, g + 1)
                    turn_p(1, 1, bk[7]).then_inc(p11_turned, 1)
                if s.on(2):
                    g, slot = t - 2, s.slot(2)
                    if s.edge:
                        if s.on(2):
                            pe.wait_ge(p0_t_ready, t - 1)
                        elif s.on(5):
                            pe.wait_ge(p10_ready, t - 4)
                        elif s.was_on(2):
                            pe.wait_ge(elu_ready, t - 2)
                    pe.wait_ge(p0_t_ready, g + 1)
                    for b in range(PAIR):
                        mm = pe.matmul(bk[5][:, b * D:(b + 1) * D], p0_t[:, b, :], hw[slot][:, b, 0:D], start=True, stop=True)
                    mm.then_inc(att0_done, 1)
                if s.on(5):
                    g = t - 5
                    if s.edge:
                        if s.on(5):
                            pe.wait_ge(p00_ready, t - 4)
                        elif s.was_on(3):
                            pe.wait_ge(k_lo_ready, t - 3)
                        elif s.was_on(5):
                            pe.wait_ge(p_t00_ready, t - 5)
                    pe.wait_ge(p00_ready, g + 1)
                    turn_p(0, 0, bk[2]).then_inc(p00_turned, 1)
                if s.on(1):
                    g, slot = t - 1, s.slot(1)
                    if s.edge:
                        if s.on(1):
                            pe.wait_ge(hw1_ready, t)
                        elif s.on(6):
                            pe.wait_ge(o_ready, t - 5)
                        elif s.was_on(1):
                            pe.wait_ge(s_sum_ready, t - 1)
                    pe.wait_ge(hw0_ready, g + 1)
                    pe.wait_ge(hw1_ready, g + 1)
                    for b in range(PAIR):
                        mm = pe.transpose(bk[6][:, b * N:(b + 1) * N], hw[slot][:, b, D + 1:D + 2].broadcast_to([P, N]), ident[:, :])
                    mm.then_inc(s2_turned, 1)
                if s.on(3):
                    g, slot = t - 3, s.slot(3)
                    if s.edge:
                        if s.on(3):
                            pe.wait_ge(h1_lo_ready, t - 2)
                        elif s.on(5):
                            pe.wait_ge(p11_ready, t - 4)
                        elif s.was_on(3):
                            pe.wait_ge(q_lo_ready, t - 3)
                    pe.wait_ge(h1_lo_ready, g + 1)
                    if s.first(3):
                        pe.wait_ge(w_ready, 1)
                    qk_product(bk[3], slot, 0).then_inc(q_done, 1)
                if s.on(3):
                    g, slot = t - 3, s.slot(3)
                    if s.on(5):
                        pe.wait_ge(p_t00_ready, t - 4)
                    elif s.was_on(3):
                        pe.wait_ge(k_lo_ready, t - 3)
                    pe.wait_ge(h1_lo_ready, g + 1)
                    if s.first(3):
                        pe.wait_ge(w_ready, 1)
                    qk_product(bk[2], slot, 1).then_inc(k_done, 1)
                if s.on(4):
                    g, slot = t - 4, s.slot(4)
                    if s.on(5):
                        pe.wait_ge(p_t10_ready, t - 4)
                    elif s.was_on(4):
                        pe.wait_ge(p01_ready, t - 4)
                    pe.wait_ge(stack_landed[slot], 12 * landed(g, slot))
                    scores(0, 1, slot, bk[4]).then_inc(scores01_done, 1)
                if s.on(5):
                    g = t - 5
                    if s.edge:
                        if s.on(5):
                            pe.wait_ge(p_t11_ready, t - 4)
                        elif s.was_on(5):
                            pe.wait_ge(inv_t_ready, t - 5)
                    pe.wait_ge(inv_ready, g + 1)
                    for k in range(PAIR * C):
                        mm = pe.transpose(bk[7][:, k * N:(k + 1) * N],
                                          inv_rep[:, k * HC:(k + 1) * HC, :].rearrange("p h d -> p (h d)"), ident[:, :])
                    mm.then_inc(inv_turned, 1)

            pipeline(pe, step)

        @block.scalar
        def _(act):
            def exp_scores(b, half, src):
                for h in range(HC):
                    hh = half * HC + h
                    ins = act.activation(p[:, b, hh, :], src[:, h * N:(h + 1) * N], ACT.Exp,
                                         bias=neg_max[:, b, hh:hh + 1], accum_out=sums[:, b, hh:hh + 1])
                return ins

            def step(s):
                t = s.t
                if s.first(0):
                    act.wait_ge(late_loaded, LATE)
                    act.activation(flat(wq_hi), flat(wq), ACT.Copy).then_inc(w_hi_ready, 1)
                if s.on(7):
                    g = t - 7
                    act.wait_ge(shift_ready[2], g + 1)
                    act.wait_ge(res_ready, g + 1)
                    for b in range(PAIR):
                        ins = act.activation(y[:, b, :], bk[1][:, b * D:(b + 1) * D], ACT.Identity, scale=rstd[2][:, b:b + 1],
                                             bias=shift[2][:, b:b + 1])
                    ins.then_inc(y_ready, 1)
                if s.on(1):
                    g = t - 1
                    act.wait_ge(z0_turned, g + 1)
                    act.activation(flat(h0_hi), bk[0][:, :], ACT.Relu).then_inc(h0_hi_ready, 1)
                if s.on(6):
                    g = t - 6
                    act.wait_ge(inv_turned, g + 1)
                    act.activation(inv_t[:, :], bk[7][:, :], ACT.Copy).then_inc(inv_t_ready, 1)
                if s.on(5):
                    g = t - 5
                    act.wait_ge(max01_ready, g + 1)
                    exp_scores(0, 1, bk[4]).then_inc(p01_ready, 1)
                if s.on(5):
                    g = t - 5
                    act.wait_ge(max10_ready, g + 1)
                    exp_scores(1, 0, bk[5]).then_inc(p10_ready, 1)
                if s.on(2):
                    g = t - 2
                    act.wait_ge(max0_ready, g + 1)
                    for b in range(PAIR):
                        ins = act.activation(p0[:, b, :], masked[:, b, :], ACT.Exp, bias=neg_max0[:, b:b + 1],
                                             accum_out=sum0[:, b:b + 1])
                    ins.then_inc(p0_ready, 1)
                if s.on(1):
                    g, slot = t - 1, s.slot(1)
                    act.wait_ge(hw0_done, g + 1)
                    act.activation(hw[slot][:, 0, :], bk[6][:, 0:DS], ACT.Copy).then_inc(hw0_ready, 1)
                if s.on(5):
                    g = t - 5
                    act.wait_ge(max11_ready, g + 1)
                    exp_scores(1, 1, bk[3]).then_inc(p11_ready, 1)
                if s.on(5):
                    g = t - 5
                    act.wait_ge(max00_ready, g + 1)
                    exp_scores(0, 0, bk[2]).then_inc(p00_ready, 1)
                if s.on(3):
                    g, slot = t - 3, s.slot(3)
                    act.wait_ge(z1_turned, g + 1)
                    act.activation(flat(h1_hi[slot]), bk[3][:, :], ACT.Relu).then_inc(h1_hi_ready, 1)
                if s.on(1):
                    g, slot = t - 1, s.slot(1)
                    act.wait_ge(hw1_done, g + 1)
                    act.activation(hw[slot][:, 1, :], bk[6][:, 0:DS], ACT.Copy).then_inc(hw1_ready, 1)
                if s.on(5):
                    g = t - 5
                    act.wait_ge(p11_turned, g + 1)
                    act.activation(turned_p(1, 1), bk[7][:, :], ACT.Copy).then_inc(p_t11_ready, 1)
                if s.on(5):
                    g = t - 5
                    act.wait_ge(p10_turned, g + 1)
                    act.activation(turned_p(1, 0), bk[4][:, :], ACT.Copy).then_inc(p_t10_ready, 1)
                if s.on(2):
                    g = t - 2
                    act.wait_ge(att0_done, g + 1)
                    for b in range(PAIR):
                        ins = act.activation(exp_h[:, b, :], bk[5][:, b * D:(b + 1) * D], ACT.Exp, scale=inv_sum0[:, b:b + 1])
                    ins.then_inc(exp_ready, 1)
                if s.on(4):
                    g, slot = t - 4, s.slot(4)
                    act.wait_ge(v_done, g + 1)
                    act.activation(v[slot][:, :, :].rearrange("p b d -> p (b d)"), bk[0][:, :], ACT.Copy).then_inc(v_ready, 1)
                if s.on(3):
                    g, slot = t - 3, s.slot(3)
                    act.wait_ge(q_done, g + 1)
                    act.activation(flat4(qk[slot][:, 0, :, :]), bk[3][:, :], ACT.Copy, scale=SCALE).then_inc(q_hi_ready, 1)
                if s.on(1):
                    g, slot = t - 1, s.slot(1)
                    act.wait_ge(s2_turned, g + 1)
                    for b in range(PAIR):
                        ins = act.activation(s_sum[:, b, :], bk[6][:, b * N:(b + 1) * N], ACT.Identity, bias=hw[slot][:, b, D:D + 1])
                    ins.then_inc(s_sum_ready, 1)
                if s.on(3):
                    g, slot = t - 3, s.slot(3)
                    act.wait_ge(k_done, g + 1)
                    act.activation(flat4(qk[slot][:, 2, :, :]), bk[2][:, :], ACT.Copy).then_inc(k_hi_ready, 1)

            pipeline(act, step)

        @block.vector
        def _(dve):
            def prepare_gat():
                dve.wait_ge(early_loaded, EARLY)
                n = 0
                for k in range(2):
                    for c in range(C):
                        if n:
                            dve.wait_ge(w_steps, n)
                        dve.tensor_tensor_reduce(a_scratch[:, :], wx[:, c, 0:D], a_rows[:, k, :], 1.0, 0.0, ALU.mult,
                                                 ALU.add, wx[:, c, D + k:D + k + 1]).then_inc(w_steps, 1)
                        n += 1
                dve.wait_ge(w_steps, n)
                dve.tensor_copy(wx_hi[:, :, :], wx[:, :, :]).then_inc(w_steps, 1)
                dve.wait_ge(w_steps, n + 1)
                dve.tensor_tensor(wx_lo[:, :, :], wx[:, :, :], wx_hi[:, :, :].bitcast(F32),
                                  ALU.subtract).then_inc(wx_ready, 1)
                dve.tensor_scalar(mask_add[:, :], adj_sb[:, :], 0.0, MASKED, ALU.is_equal, ALU.mult).then_inc(mask_ready, 1)

            def split_bias():
                dve.wait_ge(late_loaded, LATE)
                dve.memset(bias_pick[:, :], 1.0 / 32)
                dve.tensor_copy(bias_parts[0:32, :], bias_rows[0:32, :])
                dve.tensor_copy(bias_cast[:, 0, :], bias_rows[:, :]).then_inc(bias_steps, 1)
                dve.wait_ge(bias_steps, 1)
                dve.tensor_tensor(bias_rest[:, 0, :], bias_rows[:, :], bias_cast[:, 0, :],
                                  ALU.subtract).then_inc(bias_steps, 1)
                dve.wait_ge(bias_steps, 2)
                dve.tensor_copy(bias_parts[32:64, :], bias_rest[32:64, 0, :])
                dve.tensor_copy(bias_cast[:, 1, :], bias_rest[:, 0, :]).then_inc(bias_steps, 1)
                dve.wait_ge(bias_steps, 3)
                dve.tensor_tensor(bias_rest[:, 1, :], bias_rest[:, 0, :], bias_cast[:, 1, :],
                                  ALU.subtract).then_inc(bias_steps, 1)
                dve.wait_ge(bias_steps, 4)
                dve.tensor_copy(bias_parts[64:96, :], bias_rest[64:96, 1, :]).then_inc(bias_ready, 1)

            def layer_stats(k, g, src):
                for b in range(PAIR):
                    ins = dve.bn_stats(stats[k][:, b, :], src(b))
                ins.then_inc(stats_ready[k], 1)
                dve.wait_ge(stats_ready[k], g + 1)
                dve.memset(beat[:, :], 0.0)
                for b in range(PAIR):
                    ins = dve.bn_aggr(moments[k][:, b, :], stats[k][:, b, :])
                ins.then_inc(moments_ready[k], 1)

            def maxima(b, half, src):
                return dve.tensor_reduce(neg_max[:, b, half * HC:(half + 1) * HC],
                                         src[:, :].rearrange("p (h n) -> p h n", n=N), AX_X, ALU.max, negate=True)

            def rest(lo, src, hi, op, scalar):
                return dve.scalar_tensor_tensor(out=flat4(lo), in0=src, scalar=scalar, in1=flat4(hi),
                                                op0=op, op1=ALU.subtract)

            dve.wait_ge(pool_const, 2)

            def step(s):
                t = s.t
                if s.on(2):
                    g = t - 2
                    dve.wait_ge(s_sum_ready, g + 1)
                    dve.scalar_tensor_tensor(out=leaky[:, :, :], in0=s_sum[:, :, :], scalar=LEAKY_SLOPE, in1=s_sum[:, :, :],
                                             op0=ALU.mult, op1=ALU.max).then_inc(leaky_ready, 1)
                if s.on(5):
                    g = t - 5
                    dve.wait_ge(scores01_done, g + 1)
                    maxima(0, 1, bk[4]).then_inc(max01_ready, 1)
                if s.on(4):
                    g, slot = t - 4, s.slot(4)
                    dve.wait_ge(k_hi_ready, g + 1)
                    dve.tensor_tensor(flat4(qk[slot][:, 3, :, :]), bk[2][:, :], flat4(qk[slot][:, 2, :, :]),
                                      ALU.subtract).then_inc(k_lo_ready, 1)
                if s.on(5):
                    g = t - 5
                    dve.wait_ge(scores10_done, g + 1)
                    maxima(1, 0, bk[5]).then_inc(max10_ready, 1)
                if s.on(1):
                    g = t - 1
                    dve.wait_ge(h0_hi_ready, g + 1)
                    rest(h0_lo[:, :, :], bk[0][:, :], h0_hi[:, :, :].bitcast(F32), ALU.max, 0.0).then_inc(h0_lo_ready, 1)
                if s.on(3):
                    g = t - 3
                    dve.wait_ge(x1_ready, g + 1)
                    layer_stats(1, g, lambda b: x1[:, b * D:(b + 1) * D])
                if s.on(6):
                    g = t - 6
                    dve.wait_ge(av_done, g + 1)
                    dve.wait_ge(inv_t_ready, g + 1)
                    dve.tensor_tensor(o_t[:, :], bk[6][:, :], inv_t[:, :], ALU.mult).then_inc(o_ready, 1)
                if s.on(2):
                    g = t - 2
                    dve.wait_ge(masked_ready, g + 1)
                    dve.tensor_reduce(neg_max0[:, :], masked[:, :, :], AX_X, ALU.max, negate=True).then_inc(max0_ready, 1)
                if s.on(5):
                    g = t - 5
                    dve.wait_ge(scores11_done, g + 1)
                    maxima(1, 1, bk[3]).then_inc(max11_ready, 1)
                if s.on(7):
                    g, slot = t - 7, s.slot(7)
                    dve.wait_ge(out_stored[slot], landed(g, slot))
                    dve.wait_ge(y_gamma_ready, g + 1)
                    dve.tensor_tensor(out_sb[slot][:, :], y_gamma[:, :, :].rearrange("p b d -> p (b d)"), res[:, :],
                                      ALU.add).then_inc(out_ready, 1)
                if s.on(5):
                    g = t - 5
                    dve.wait_ge(scores00_done, g + 1)
                    maxima(0, 0, bk[2]).then_inc(max00_ready, 1)
                if s.on(0):
                    g, slot = t, s.slot(0)
                    dve.wait_ge(x_loaded[slot], landed(g, slot))
                    layer_stats(0, g, lambda b: xs_of(g, b))
                    if s.first(0):
                        prepare_gat()
                if s.on(2):
                    g = t - 2
                    dve.wait_ge(p0_ready, g + 1)
                    dve.tensor_scalar(beta_sum0[:, :], sum0[:, :], gbeta[:, 0:1], None, ALU.mult)
                    dve.reciprocal(inv_sum0[:, :], sum0[:, :]).then_inc(inv0_ready, 1)
                if s.on(6):
                    g = t - 6
                    dve.wait_ge(proj_done, g + 1)
                    layer_stats(2, g, lambda b: bk[1][:, b * D:(b + 1) * D])
                if s.on(5):
                    g = t - 5
                    dve.wait_ge(p01_turned, g + 1)
                    dve.tensor_copy(turned_p(0, 1), bk[7][:, :]).then_inc(p_t01_ready, 1)
                if s.on(2):
                    g = t - 2
                    dve.wait_ge(p0_turned, g + 1)
                    dve.wait_ge(inv0_ready, g + 1)
                    for b in range(PAIR):
                        ins = dve.scalar_tensor_tensor(out=p0_t[:, b, :], in0=ident[:, :], scalar=beta_sum0[:, b:b + 1],
                                                       in1=bk[5][:, b * N:(b + 1) * N], op0=ALU.mult, op1=ALU.add)
                    ins.then_inc(p0_t_ready, 1)
                if s.on(6):
                    g = t - 6
                    dve.wait_ge(proj_done, g + 1)
                    dve.wait_ge(x1b_ready, g + 1)
                    dve.tensor_tensor(res[:, :], bk[1][:, :], xs_of(g), ALU.add).then_inc(res_ready, 1)
                if s.on(3):
                    g, slot = t - 3, s.slot(3)
                    dve.wait_ge(h1_hi_ready, g + 1)
                    rest(h1_lo[slot][:, :, :], bk[3][:, :], h1_hi[slot][:, :, :].bitcast(F32), ALU.max, 0.0).then_inc(h1_lo_ready, 1)
                if s.on(5):
                    g = t - 5
                    dve.wait_ge(p00_ready, g + 1)
                    dve.wait_ge(p01_ready, g + 1)
                    dve.wait_ge(p10_ready, g + 1)
                    dve.wait_ge(p11_ready, g + 1)
                    dve.reciprocal(inv_sum[:, :], sums[:, :, :].rearrange("p b h -> p (b h)")).then_inc(recip_done, 1)
                    dve.wait_ge(recip_done, g + 1)
                    dve.tensor_copy(inv_rep[:, :, :], inv_sum[:, :].unsqueeze(2).broadcast_to([P, PAIR * H, HD])).then_inc(inv_ready, 1)
                if s.on(5):
                    g = t - 5
                    dve.wait_ge(p00_turned, g + 1)
                    dve.tensor_copy(turned_p(0, 0), bk[2][:, :]).then_inc(p_t00_ready, 1)
                if s.on(2):
                    g = t - 2
                    dve.wait_ge(exp_ready, g + 1)
                    dve.tensor_scalar(exp_m1[:, :, :], exp_h[:, :, :], 1.0, 1.0, ALU.min, ALU.subtract).then_inc(exp_m1_ready, 1)
                if s.on(2):
                    g = t - 2
                    dve.wait_ge(exp_m1_ready, g + 1)
                    for b in range(PAIR):
                        ins = dve.scalar_tensor_tensor(out=elu[:, b * D:(b + 1) * D], in0=bk[5][:, b * D:(b + 1) * D],
                                                       scalar=inv_sum0[:, b:b + 1], in1=exp_m1[:, b, :], op0=ALU.mult, op1=ALU.max)
                    ins.then_inc(elu_ready, 1)
                if s.on(3):
                    g, slot = t - 3, s.slot(3)
                    dve.wait_ge(q_hi_ready, g + 1)
                    rest(qk[slot][:, 1, :, :], bk[3][:, :], qk[slot][:, 0, :, :], ALU.mult, SCALE).then_inc(q_lo_ready, 1)
                if s.first(1):
                    split_bias()

            pipeline(dve, step)

        @block.gpsimd
        def _(pool):
            pool.memset(minus_half[:, :], -0.5)
            pool.memset(minus_one[:, :], -1.0)
            pool.memset(eps[:, :], LN_EPS)
            pool.memset(ident[:, :], 0.0).then_inc(ident_cleared, 1)
            pool.wait_ge(ident_cleared, 1)
            pool.affine_select(out=ident[:, :], in_=ident[:, :], compare_op=ALU.not_equal, fill=1.0, base=0,
                               pattern=[[-1, P]], channel_multiplier=1).then_inc(pool_const, 1)
            pool.wait_ge(pool_const, 1)
            pool.tensor_copy(ident_bf[:, :], ident[:, :]).then_inc(pool_const, 1)
            pool.wait_ge(pool_const, 2)

            def norm(k, g):
                pool.tensor_tensor(var_eps[k][:, :], moments[k][:, :, 1], eps[:, :],
                                   ALU.add).then_inc(eps_added[k], 1)
                pool.tensor_tensor(neg_mean[k][:, :], moments[k][:, :, 0], minus_one[:, :],
                                   ALU.mult).then_inc(neg_mean_ready[k], 1)
                pool.wait_ge(eps_added[k], g + 1)
                pool.tensor_tensor(rstd[k][:, :], var_eps[k][:, :], minus_half[:, :],
                                   ALU.pow).then_inc(rstd_ready[k], 1)
                pool.wait_ge(rstd_ready[k], g + 1)
                pool.wait_ge(neg_mean_ready[k], g + 1)
                pool.tensor_tensor(shift[k][:, :], neg_mean[k][:, :], rstd[k][:, :],
                                   ALU.mult).then_inc(shift_ready[k], 1)

            pool.wait_ge(early_loaded, EARLY)

            def step(s):
                t = s.t
                if s.on(3):
                    g = t - 3
                    if s.from_group(1, 3):
                        pool.wait_ge(x1b_ready, g)
                    pool.wait_ge(elu_ready, g + 1)
                    pool.tensor_tensor(pool_beat[:, :], eps[:, :], eps[:, :], ALU.add)
                    pool.tensor_tensor(x1[:, :], elu[:, :], xs_of(g), ALU.add).then_inc(x1_ready, 1)
                if s.on(7):
                    g = t - 7
                    pool.wait_ge(y_ready, g + 1)
                    pool.tensor_tensor(y_gamma[:, :, :], y[:, :, :], gamma[:, :].unsqueeze(1).broadcast_to([P, PAIR, D]),
                                       ALU.mult).then_inc(y_gamma_ready, 1)
                if s.on(2):
                    g = t - 2
                    pool.wait_ge(leaky_ready, g + 1)
                    pool.tensor_tensor(masked[:, :, :], leaky[:, :, :], adj_sb[:, :].unsqueeze(1).broadcast_to([P, PAIR, N]),
                                       ALU.mult).then_inc(masked_ready, 1)
                if s.on(3):
                    g = t - 3
                    pool.wait_ge(moments_ready[1], g + 1)
                    norm(1, g)
                    for b in range(PAIR):
                        ins = pool.tensor_scalar(z1[:, b * D:(b + 1) * D], x1[:, b * D:(b + 1) * D], neg_mean[1][:, b:b + 1],
                                                 rstd[1][:, b:b + 1], ALU.add, ALU.mult)
                    ins.then_inc(z1_ready, 1)
                if s.on(6):
                    g = t - 6
                    pool.wait_ge(moments_ready[2], g + 1)
                    norm(2, g)
                if s.on(0):
                    g = t
                    pool.wait_ge(moments_ready[0], g + 1)
                    norm(0, g)
                    pool.tensor_tensor(pairs(centred[:, :]), pairs(xs_of(g)), neg_mean[0][:, :].unsqueeze(2).broadcast_to([P, PAIR, D]),
                                       ALU.add).then_inc(centred_ready, 1)
                    pool.wait_ge(centred_ready, g + 1)
                    pool.tensor_tensor(pairs(z0[:, :]), pairs(centred[:, :]), rstd[0][:, :].unsqueeze(2).broadcast_to([P, PAIR, D]),
                                       ALU.mult).then_inc(z0_ready, 1)
                if s.on(3):
                    g = t - 3
                    if s.first(3):
                        pool.wait_ge(late_loaded, LATE)
                    pool.tensor_tensor(pairs(xs_of(g)), pairs(x1[:, :]), lnb[:, :].unsqueeze(1).broadcast_to([P, PAIR, D]),
                                       ALU.add).then_inc(x1b_ready, 1)
                if s.first(0):
                    pool.wait_ge(w_hi_ready, 1)
                    pool.tensor_tensor(flat(wq_lo), flat(wq), flat4(wq_hi[:, :, :].bitcast(F32)),
                                       ALU.subtract).then_inc(w_ready, 1)

            pipeline(pool, step)


_INS = ['x', 'adj', 'L0_gnn_W', 'L0_gnn_a', 'L0_gnn_beta', 'L1_gnn_w_qkv', 'L1_gnn_w_proj', 'L1_gnn_b_proj',
        'L1_gnn_ln_gamma', 'L1_gnn_ln_beta']


def kernel(**inputs):
    import numpy as _np
    import concourse.bacc as _bacc
    from concourse import mybir as _mybir
    from concourse.bass_utils import run_bass_kernel_spmd as _run

    nc = _bacc.Bacc("TRN2", target_bir_lowering=False, num_devices=1)
    arrays, args = {}, []
    for name in _INS:
        a = _np.ascontiguousarray(inputs[name])
        arrays[f"in_{name}_dram"] = a
        args.append(nc.dram_tensor(f"in_{name}_dram", a.shape, _mybir.dt.from_np(a.dtype), kind="ExternalInput").ap())
    shape = inputs['x'].shape
    args.append(nc.dram_tensor("out_0_dram", shape, _mybir.dt.float32, kind="ExternalOutput").ap())
    gat_transformer(nc, *args)
    r = _run(nc, [arrays], core_ids=[0])
    return r.results[0]["out_0_dram"]
```
